# Optimizing a Trainium2 kernel written in Bass

```python
import numpy as np
import jax
import jax.numpy as jnp

def _softmax(x, axis=-1):
    return jax.nn.softmax(x, axis=axis)
def _gelu(x):
    return jax.nn.gelu(x, approximate=True)
def _silu(x):
    return jax.nn.silu(x)
def _sigmoid(x):
    return jax.nn.sigmoid(x)
def _layernorm(x, axis=-1, eps=1e-5):
    m = jnp.mean(x, axis=axis, keepdims=True)
    v = jnp.var(x, axis=axis, keepdims=True)
    return (x - m) / jnp.sqrt(v + eps)
def _scatter_add(tgt, idx, src, axis=0):
    return tgt.at[idx].add(src)
def _segment_sum(src, seg, n):
    return jax.ops.segment_sum(src, seg, n)

kernel_name = 'mk_rec_standalone_d1_rec_e25b9a'

def setup_inputs(seed: int = 0):
    np.random.seed(seed)
    _w = jnp.asarray
    def _rec_inputs():
        import jax
        import jax.numpy as jnp
        _rk = jax.random.key(seed)
        r_X = jax.random.uniform(jax.random.fold_in(_rk, 1), (16384, 39), jnp.float32, 0.0, 9999)
        r_sparse_idx = jnp.stack([jax.random.randint(jax.random.fold_in(jax.random.fold_in(_rk, 2), 0), (16384,), 0, 10000, jnp.int32), jax.random.randint(jax.random.fold_in(jax.random.fold_in(_rk, 2), 1), (16384,), 0, 10000, jnp.int32), jax.random.randint(jax.random.fold_in(jax.random.fold_in(_rk, 2), 2), (16384,), 0, 10000, jnp.int32), jax.random.randint(jax.random.fold_in(jax.random.fold_in(_rk, 2), 3), (16384,), 0, 10000, jnp.int32), jax.random.randint(jax.random.fold_in(jax.random.fold_in(_rk, 2), 4), (16384,), 0, 10000, jnp.int32), jax.random.randint(jax.random.fold_in(jax.random.fold_in(_rk, 2), 5), (16384,), 0, 10000, jnp.int32), jax.random.randint(jax.random.fold_in(jax.random.fold_in(_rk, 2), 6), (16384,), 0, 10000, jnp.int32), jax.random.randint(jax.random.fold_in(jax.random.fold_in(_rk, 2), 7), (16384,), 0, 10000, jnp.int32), jax.random.randint(jax.random.fold_in(jax.random.fold_in(_rk, 2), 8), (16384,), 0, 10000, jnp.int32), jax.random.randint(jax.random.fold_in(jax.random.fold_in(_rk, 2), 9), (16384,), 0, 10000, jnp.int32), jax.random.randint(jax.random.fold_in(jax.random.fold_in(_rk, 2), 10), (16384,), 0, 10000, jnp.int32), jax.random.randint(jax.random.fold_in(jax.random.fold_in(_rk, 2), 11), (16384,), 0, 10000, jnp.int32), jax.random.randint(jax.random.fold_in(jax.random.fold_in(_rk, 2), 12), (16384,), 0, 10000, jnp.int32), jax.random.randint(jax.random.fold_in(jax.random.fold_in(_rk, 2), 13), (16384,), 0, 10000, jnp.int32), jax.random.randint(jax.random.fold_in(jax.random.fold_in(_rk, 2), 14), (16384,), 0, 10000, jnp.int32), jax.random.randint(jax.random.fold_in(jax.random.fold_in(_rk, 2), 15), (16384,), 0, 10000, jnp.int32), jax.random.randint(jax.random.fold_in(jax.random.fold_in(_rk, 2), 16), (16384,), 0, 10000, jnp.int32), jax.random.randint(jax.random.fold_in(jax.random.fold_in(_rk, 2), 17), (16384,), 0, 10000, jnp.int32), jax.random.randint(jax.random.fold_in(jax.random.fold_in(_rk, 2), 18), (16384,), 0, 10000, jnp.int32), jax.random.randint(jax.random.fold_in(jax.random.fold_in(_rk, 2), 19), (16384,), 0, 9999, jnp.int32), jax.random.randint(jax.random.fold_in(jax.random.fold_in(_rk, 2), 20), (16384,), 0, 10000, jnp.int32), jax.random.randint(jax.random.fold_in(jax.random.fold_in(_rk, 2), 21), (16384,), 0, 10000, jnp.int32), jax.random.randint(jax.random.fold_in(jax.random.fold_in(_rk, 2), 22), (16384,), 0, 10000, jnp.int32), jax.random.randint(jax.random.fold_in(jax.random.fold_in(_rk, 2), 23), (16384,), 0, 10000, jnp.int32), jax.random.randint(jax.random.fold_in(jax.random.fold_in(_rk, 2), 24), (16384,), 0, 10000, jnp.int32), jax.random.randint(jax.random.fold_in(jax.random.fold_in(_rk, 2), 25), (16384,), 0, 10000, jnp.int32)], axis=1)
        return r_X, r_sparse_idx
    r_X, r_sparse_idx = _rec_inputs()
    def _L0_rec_setup():
        import jax, jax.numpy as jnp
        import numpy as np
        B = 32768
        N_SPARSE = 26
        N_DENSE = 13
        VOCAB = 10000
        E = 64
        H = 2
        L = 3
        DH = E // H
        DNN_IN = N_DENSE + N_SPARSE * E
        H1, H2 = (256, 128)

        def _split_heads(x):
            b, f, _ = x.shape
            return jnp.moveaxis(x.reshape(b, f, H, DH), 2, 0)

        def _interacting_layer(att, wq, wk, wv, wres):
            q = _split_heads(jnp.einsum('bfe,eo->bfo', att, wq))
            k = _split_heads(jnp.einsum('bfe,eo->bfo', att, wk))
            v = _split_heads(jnp.einsum('bfe,eo->bfo', att, wv))
            scores = jnp.einsum('hbik,hbjk->hbij', q, k)
            attn = jax.nn.softmax(scores, axis=-1)
            out = jnp.einsum('hbij,hbjd->hbid', attn, v)
            b, f = (att.shape[0], att.shape[1])
            out = jnp.moveaxis(out, 0, 2).reshape(b, f, E)
            out = out + jnp.einsum('bfe,eo->bfo', att, wres)
            return jax.nn.relu(out)
        key = jax.random.key(seed)
        ks = jax.random.split(key, 12)
        sparse_idx = jax.random.randint(ks[0], (B, N_SPARSE), 0, VOCAB, dtype=jnp.int32)
        dense = jax.random.uniform(ks[1], (B, N_DENSE), dtype=jnp.float32)
        X = jnp.concatenate([sparse_idx.astype(jnp.float32), dense], axis=1)
        emb_tables = jax.random.normal(ks[2], (N_SPARSE, VOCAB, E), dtype=jnp.float32)
        Wq = jax.random.normal(ks[3], (L, E, E), dtype=jnp.float32) * 0.05
        Wk = jax.random.normal(ks[4], (L, E, E), dtype=jnp.float32) * 0.05
        Wv = jax.random.normal(ks[5], (L, E, E), dtype=jnp.float32) * 0.05
        Wres = jax.random.normal(ks[6], (L, E, E), dtype=jnp.float32) * 0.05
        dnn_W1 = jax.random.normal(ks[7], (DNN_IN, H1), dtype=jnp.float32) * 0.0001
        dnn_b1 = jnp.zeros((H1,), dtype=jnp.float32)
        dnn_W2 = jax.random.normal(ks[8], (H1, H2), dtype=jnp.float32) * 0.0001
        dnn_b2 = jnp.zeros((H2,), dtype=jnp.float32)
        out_W = jax.random.normal(ks[9], (N_SPARSE * E + H2, 1), dtype=jnp.float32) * 1e-05
        lin_W = jax.random.normal(ks[10], (N_SPARSE + N_DENSE, 1), dtype=jnp.float32) * 1e-05
        lin_b = jnp.zeros((1,), dtype=jnp.float32)
        return {'X': X, 'sparse_idx': sparse_idx, 'emb_tables': emb_tables, 'Wq': Wq, 'Wk': Wk, 'Wv': Wv, 'Wres': Wres, 'dnn_W1': dnn_W1, 'dnn_b1': dnn_b1, 'dnn_W2': dnn_W2, 'dnn_b2': dnn_b2, 'out_W': out_W, 'lin_W': lin_W, 'lin_b': lin_b}
    _L0_rec_all = _L0_rec_setup()
    _L0_rec_in = {k: v for k, v in _L0_rec_all.items() if k in ('emb_tables', 'Wq', 'Wk', 'Wv', 'Wres', 'dnn_W1', 'dnn_b1', 'dnn_W2', 'dnn_b2', 'out_W', 'lin_W', 'lin_b', )}
    del _L0_rec_all

    return {
        "r_X": r_X,
        "r_sparse_idx": r_sparse_idx,
        "L0_rec_emb_tables": _L0_rec_in["emb_tables"],
        "L0_rec_Wq": _L0_rec_in["Wq"],
        "L0_rec_Wk": _L0_rec_in["Wk"],
        "L0_rec_Wv": _L0_rec_in["Wv"],
        "L0_rec_Wres": _L0_rec_in["Wres"],
        "L0_rec_dnn_W1": _L0_rec_in["dnn_W1"],
        "L0_rec_dnn_b1": _L0_rec_in["dnn_b1"],
        "L0_rec_dnn_W2": _L0_rec_in["dnn_W2"],
        "L0_rec_dnn_b2": _L0_rec_in["dnn_b2"],
        "L0_rec_out_W": _L0_rec_in["out_W"],
        "L0_rec_lin_W": _L0_rec_in["lin_W"],
        "L0_rec_lin_b": _L0_rec_in["lin_b"],
    }

def reference(r_X, r_sparse_idx, L0_rec_emb_tables, L0_rec_Wq, L0_rec_Wk, L0_rec_Wv, L0_rec_Wres, L0_rec_dnn_W1, L0_rec_dnn_b1, L0_rec_dnn_W2, L0_rec_dnn_b2, L0_rec_out_W, L0_rec_lin_W, L0_rec_lin_b):
    import jax
    import jax.numpy as jnp
    def _L0_rec_ref(X, sparse_idx, emb_tables, Wq, Wk, Wv, Wres, dnn_W1, dnn_b1, dnn_W2, dnn_b2, out_W, lin_W, lin_b):
        import jax, jax.numpy as jnp
        import numpy as np
        B = 32768
        N_SPARSE = 26
        N_DENSE = 13
        VOCAB = 10000
        E = 64
        H = 2
        L = 3
        DH = E // H
        DNN_IN = N_DENSE + N_SPARSE * E
        H1, H2 = (256, 128)

        def _split_heads(x):
            b, f, _ = x.shape
            return jnp.moveaxis(x.reshape(b, f, H, DH), 2, 0)

        def _interacting_layer(att, wq, wk, wv, wres):
            q = _split_heads(jnp.einsum('bfe,eo->bfo', att, wq))
            k = _split_heads(jnp.einsum('bfe,eo->bfo', att, wk))
            v = _split_heads(jnp.einsum('bfe,eo->bfo', att, wv))
            scores = jnp.einsum('hbik,hbjk->hbij', q, k)
            attn = jax.nn.softmax(scores, axis=-1)
            out = jnp.einsum('hbij,hbjd->hbid', attn, v)
            b, f = (att.shape[0], att.shape[1])
            out = jnp.moveaxis(out, 0, 2).reshape(b, f, E)
            out = out + jnp.einsum('bfe,eo->bfo', att, wres)
            return jax.nn.relu(out)
        logit = jax.nn.relu(X @ lin_W + lin_b)
        emb = emb_tables[jnp.arange(N_SPARSE), sparse_idx]
        att = emb
        for l in range(L):
            att = _interacting_layer(att, Wq[l], Wk[l], Wv[l], Wres[l])
        att_flat = att.reshape(att.shape[0], -1)
        sparse_flat = emb.reshape(emb.shape[0], -1)
        dense_input = X[:, N_SPARSE:]
        dnn_in = jnp.concatenate([dense_input, sparse_flat], axis=1)
        h = jax.nn.relu(dnn_in @ dnn_W1 + dnn_b1)
        h = jax.nn.relu(h @ dnn_W2 + dnn_b2)
        stack = jnp.concatenate([att_flat, h], axis=-1)
        logit = logit + stack @ out_W
        return jax.nn.sigmoid(logit)

    y = _L0_rec_ref(r_X, r_sparse_idx, L0_rec_emb_tables, L0_rec_Wq, L0_rec_Wk, L0_rec_Wv, L0_rec_Wres, L0_rec_dnn_W1, L0_rec_dnn_b1, L0_rec_dnn_W2, L0_rec_dnn_b2, L0_rec_out_W, L0_rec_lin_W, L0_rec_lin_b)
    return y


_drawn_inputs = setup_inputs


def setup_inputs(seed=0):
    import zlib

    import numpy as np

    out = dict(_drawn_inputs(seed))
    spreads = {'L0_rec_dnn_b1': (0.0, 2.0), 'L0_rec_dnn_b2': (0.0, 2.0)}
    factors = {'r_X': 2.747,
     'L0_rec_emb_tables': 8.0,
     'L0_rec_Wq': 8.0,
     'L0_rec_Wk': 8.0,
     'L0_rec_Wv': 8.0,
     'L0_rec_Wres': 8.0,
     'L0_rec_dnn_W1': 200.0,
     'L0_rec_dnn_W2': 200.0,
     'L0_rec_out_W': 8.0,
     'L0_rec_lin_W': 2.719}
    for name, (base, spread) in spreads.items():
        noise = np.random.default_rng([zlib.crc32(name.encode()), seed]).standard_normal(out[name].shape)
        drawn = base * np.exp(spread * noise) if base else spread * noise
        out[name] = jnp.asarray(drawn.astype(out[name].dtype))
    for name, factor in factors.items():
        out[name] = (out[name] * factor).astype(out[name].dtype)
    return out
```

```python
import numpy as np
import concourse.bass as bass
from concourse import mybir
from contextlib import ExitStack

BATCH, FIELDS, DENSE, VOCAB, EMB = 16384, 26, 13, 10000, 64
HEADS, LAYERS, HIDDEN1, HIDDEN2 = 2, 3, 256, 128
FEATURES = FIELDS + DENSE
HD = EMB // HEADS
PE_ROWS = 128
FP = 32
PAIRS = 128
EXAMPLES = 2 * PAIRS
ITERATIONS = BATCH // EXAMPLES
CHUNK = 16
CHUNKS = PAIRS // CHUNK
QUADS = CHUNK // 4
BLOCKS = 4
COLS = CHUNK * FIELDS
QCOLS = 4 * FIELDS
UNITS = LAYERS * CHUNKS
PROJ, SCORE = 3, 2
TURN = 4
VSLOTS = 4
FIELDS_PER_SLOT = 7
DNN_SLOTS = 4
H1_SLOT, L2_SLOT, X0_SLOT = 8, 11, 12
FINAL_SLOT, SUM_SLOT, SIGMOID_SLOT = 1, 2, 3


def interacting_attention_recommender(nc, table, idx, offs, xt, wq, wk, wv, wr, w1, b1, w2, b2,
                                      ow_att, ow_dnn, lw, lb, out):
    fp32, i32 = mybir.dt.float32, mybir.dt.int32
    ALU = mybir.AluOpType
    ACT = mybir.ActivationFunctionType
    AX = mybir.AxisListType.X

    ctx = ExitStack()
    with ctx:
        def sb(name, shape, dt=fp32):
            return ctx.enter_context(nc.sbuf_tensor(name, shape, dt))

        def bank(name):
            return ctx.enter_context(nc.psum_tensor(name, [PE_ROWS, 512], fp32))

        def sem(name):
            return ctx.enter_context(nc.semaphore(name))

        w_att = sb("w_att", [PE_ROWS, LAYERS, 4, PE_ROWS])
        w1_emb = sb("w1_emb", [PE_ROWS, FIELDS, HIDDEN1])
        w1_den = sb("w1_den", [PE_ROWS, HIDDEN1])
        w2_sb = sb("w2_sb", [PE_ROWS, 2, HIDDEN2])
        b1_sb = sb("b1_sb", [PE_ROWS, 2])
        b2_sb = sb("b2_sb", [PE_ROWS, 1])
        ow_att_sb = sb("ow_att_sb", [PE_ROWS, FIELDS])
        ow_dnn_sb = sb("ow_dnn_sb", [PE_ROWS, 2, 2])
        lw_sb = sb("lw_sb", [FEATURES, 2, 2])
        lb_sb = sb("lb_sb", [2, 1])
        pick = sb("pick", [PE_ROWS, 2])
        ident = sb("ident", [PE_ROWS, PE_ROWS])
        idx_all = sb("idx_all", [QCOLS, ITERATIONS, PAIRS // 4 * 2], i32)
        offs_sb = sb("offs_sb", [QCOLS, 1], i32)
        idx_now = sb("idx_now", [QCOLS, PAIRS // 4 * 2], i32)
        rows = sb("rows", [QCOLS, PAIRS // 4, PE_ROWS])
        x0 = sb("x0", [PE_ROWS, CHUNKS, CHUNK, FP])
        x = sb("x", [PE_ROWS, CHUNKS, CHUNK, FP])
        q_sb = [sb(f"q_sb{i}", [PE_ROWS, CHUNK, FP]) for i in range(2)]
        k_bd = [sb(f"k_bd{i}", [PE_ROWS, CHUNK, BLOCKS, FIELDS]) for i in range(2)]
        v_sb = [sb(f"v_sb{i}", [PE_ROWS, QUADS, PE_ROWS]) for i in range(VSLOTS)]
        e_sb = [sb(f"e_sb{i}", [PE_ROWS, QUADS * BLOCKS, FIELDS]) for i in range(2)]
        p_sb = sb("p_sb", [PE_ROWS, QUADS * BLOCKS, FP])
        pt_bd = [sb(f"pt_bd{i}", [PE_ROWS, QUADS * BLOCKS, 4, FP]) for i in range(2)]
        row_max = sb("row_max", [PE_ROWS, QUADS * BLOCKS])
        row_sum = sb("row_sum", [PE_ROWS, QUADS * BLOCKS])
        row_inv = sb("row_inv", [PE_ROWS, QUADS * BLOCKS])
        weighed = sb("weighed", [PE_ROWS, CHUNK, FIELDS])
        att_part = sb("att_part", [PE_ROWS, PAIRS])
        x_den = sb("x_den", [PE_ROWS, PAIRS])
        x_all = sb("x_all", [FEATURES, 2, PAIRS])
        h1 = sb("h1", [PE_ROWS, 2, 2, PAIRS])
        h2 = sb("h2", [PE_ROWS, 2, PAIRS])
        lin = sb("lin", [2, PAIRS])
        logit = sb("logit", [2, PAIRS])
        expneg = sb("expneg", [2, PAIRS])
        denom = sb("denom", [2, PAIRS])
        result = sb("result", [2, PAIRS])

        q_ps, k_ps, v_ps, s_ps, o_ps, t_ps = (bank(n) for n in ("q_ps", "k_ps", "v_ps", "s_ps", "o_ps", "t_ps"))
        d_ps = [bank("d_ps0"), bank("d_ps1")]

        w_zeroed = sem("w_zeroed")
        buf_zeroed = sem("buf_zeroed")
        ident_ready = sem("ident_ready")
        att_w_loaded = sem("att_w_loaded")
        dnn_w_loaded = sem("dnn_w_loaded")
        idx_loaded = sem("idx_loaded")
        idx_ready = sem("idx_ready")
        gathered = [sem(f"gathered{c}") for c in range(CHUNKS)]
        x_den_loaded = sem("x_den_loaded")
        x_all_loaded = sem("x_all_loaded")
        xt_done = sem("xt_done")
        x0_ready = sem("x0_ready")
        q_done, k_done, v_done = sem("q_done"), sem("k_done"), sem("v_done")
        q_ready, k_ready, v_ready = sem("q_ready"), sem("k_ready"), sem("v_ready")
        s_done = sem("s_done")
        max_done, sub_done = sem("max_done"), sem("sub_done")
        exp_done = sem("exp_done")
        sum_done, inv_done, p_ready = sem("sum_done"), sem("inv_done"), sem("p_ready")
        pt_ready = sem("pt_ready")
        o_done = sem("o_done")
        x_ready = sem("x_ready")
        weighed_done, att_done = sem("weighed_done"), sem("att_done")
        dnn_done = sem("dnn_done")
        h1_ready = sem("h1_ready")
        l2_done = sem("l2_done")
        h2_ready = sem("h2_ready")
        final_done = sem("final_done")
        lin_ready, logit_ready, expneg_ready = sem("lin_ready"), sem("logit_ready"), sem("expneg_ready")
        denom_ready, result_ready = sem("denom_ready"), sem("result_ready")
        stored = sem("stored")
        cleared, sp_cleared = sem("cleared"), sem("sp_cleared")

        def unit(it, s):
            n = it * UNITS + s
            return s % UNITS, n, not isinstance(n, int) or 0 <= n < ITERATIONS * UNITS

        def turn(it, s, back=0):
            i = it + (s // UNITS - back)
            return i, not isinstance(i, int) or 0 <= i < ITERATIONS

        def wait(eng, semaphore, value):
            if not isinstance(value, int) or value > 0:
                eng.wait_ge(semaphore, value)

        def over_slots(eng, slot):
            for s in range(-PROJ, TURN):
                slot(0, s)
            with eng.Fori(0, ITERATIONS - 1) as it:
                for s in range(TURN, TURN + UNITS):
                    slot(it, s)
            for s in range(TURN, TURN + UNITS):
                slot(ITERATIONS - 1, s)

        block = ctx.enter_context(nc.Block())

        @block.sync
        def _(sp):
            sp.dma_start(idx_all[:, :, :], idx).then_inc(idx_loaded, 16)
            sp.dma_start(offs_sb[:, :], offs).then_inc(idx_loaded, 16)
            sp.wait_ge(w_zeroed, 3)
            for kind, w in enumerate((wq, wk, wv, wr)):
                for e in range(2):
                    half = slice(EMB * e, EMB * e + EMB)
                    sp.dma_start(w_att[half, :, kind, half], w.rearrange("l f o -> f l o")).then_inc(att_w_loaded, 16)
            for e in range(2):
                half = slice(EMB * e, EMB * e + EMB)
                sp.dma_start(w1_emb[half, :, :], w1[DENSE:, :].rearrange("(i f) o -> f i o", f=EMB)).then_inc(dnn_w_loaded, 16)
                sp.dma_start(w1_den[EMB * e:EMB * e + DENSE, :], w1[0:DENSE, :]).then_inc(dnn_w_loaded, 16)
                sp.dma_start(x_den[EMB * e:EMB * e + DENSE, :], xt[0, FIELDS:, e, :]).then_inc(x_den_loaded, 16)
                sp.dma_start(ow_att_sb[half, :], ow_att).then_inc(dnn_w_loaded, 16)
                sp.dma_start(ow_dnn_sb[:, e, e:e + 1], ow_dnn).then_inc(dnn_w_loaded, 16)
                sp.dma_start(lw_sb[:, e, e:e + 1], lw).then_inc(dnn_w_loaded, 16)
                sp.dma_start(lb_sb[e:e + 1, :], lb).then_inc(dnn_w_loaded, 16)
            sp.dma_start(w2_sb[:, :, :], w2.rearrange("(k p) o -> p k o", p=PE_ROWS)).then_inc(dnn_w_loaded, 16)
            sp.dma_start(b1_sb[:, :], b1).then_inc(dnn_w_loaded, 16)
            sp.dma_start(b2_sb[:, :], b2).then_inc(dnn_w_loaded, 16)
            sp.dma_start(x_all[:, :, :], xt[0]).then_inc(x_all_loaded, 16)

            def store(it):
                sp.wait_ge(result_ready, it + 1)
                sp.sem_inc(sp_cleared, 1)
                sp.dma_start(out[it], result[:, :]).then_inc(stored, 16)

            with sp.Fori(0, ITERATIONS - 1) as it:
                sp.wait_ge(dnn_done, it + 1)
                sp.sem_inc(sp_cleared, 1)
                for e in range(2):
                    sp.dma_start(x_den[EMB * e:EMB * e + DENSE, :], xt[it + 1, FIELDS:, e, :]).then_inc(x_den_loaded, 16)
                sp.wait_ge(final_done, it + 1)
                sp.sem_inc(sp_cleared, 1)
                sp.dma_start(x_all[:, :, :], xt[it + 1]).then_inc(x_all_loaded, 16)
                store(it)
            store(ITERATIONS - 1)
            sp.wait_ge(stored, 16 * ITERATIONS)

        @block.gpsimd
        def _(pool):
            pool.memset(w_att[:, :, :, :], 0.0).then_inc(w_zeroed, 1)
            pool.memset(ow_dnn_sb[:, :, :], 0.0).then_inc(w_zeroed, 1)
            pool.memset(lw_sb[:, :, :], 0.0).then_inc(w_zeroed, 1)
            pool.memset(ident[:, :], 0.0).then_inc(ident_ready, 1)
            pool.wait_ge(ident_ready, 1)
            pool.affine_select(out=ident[:, :], in_=ident[:, :], compare_op=ALU.not_equal, fill=1.0,
                               base=0, pattern=[[-1, PE_ROWS]], channel_multiplier=1).then_inc(ident_ready, 1)
            pool.wait_ge(idx_loaded, 32)

            def gather(it, first):
                if not first:
                    for c in range(CHUNKS):
                        pool.wait_ge(gathered[c], it * (16 * 2 * QUADS))
                pool.tensor_tensor(idx_now[:, :], idx_all[:, it, :], offs_sb[:, :].to_broadcast([QCOLS, PAIRS // 4 * 2]),
                                   ALU.add).then_inc(idx_ready, 1)
                pool.wait_ge(idx_ready, it + 1)
                pool.sem_inc(cleared, 1)
                for c in range(CHUNKS):
                    if not first:
                        pool.wait_ge(xt_done, it * CHUNKS + (c + 1 - CHUNKS))
                    pool.sem_inc(cleared, 1)
                    for g in range(c * QUADS, (c + 1) * QUADS):
                        for e in range(2):
                            pool.indirect_dma_start(
                                out=rows[:, g, EMB * e:EMB * e + EMB], out_offset=None, in_=table,
                                in_offset=bass.IndirectOffsetOnAxis(ap=idx_now[:, 2 * g + e:2 * g + e + 1], axis=0),
                            ).then_inc(gathered[c], 16)

            gather(0, True)
            with pool.Fori(1, ITERATIONS) as it:
                gather(it, False)

        @block.tensor
        def _(pe):
            def embed(it, c):
                wait(pe, gathered[c], (it + 1) * (16 * 2 * QUADS))
                wait(pe, x0_ready, it * CHUNKS + c)
                for g in range(QUADS):
                    last = pe.transpose(t_ps[:, g * QCOLS:(g + 1) * QCOLS], rows[:, c * QUADS + g, :], ident[0:QCOLS, 0:QCOLS])
                last.then_inc(xt_done, 1)

            pe.wait_ge(ident_ready, 2)
            for c in range(CHUNKS):
                embed(0, c)
            pe.wait_ge(att_w_loaded, 16 * 8)
            pe.wait_ge(dnn_w_loaded, 16 * 15)

            def slot(it, s):
                u, n, there = unit(it, s + PROJ)
                if there:
                    l, c = divmod(u, CHUNKS)
                    src = x if l else x0
                    if l:
                        wait(pe, x_ready, n + (1 - CHUNKS))
                    else:
                        wait(pe, x0_ready, turn(it, s + PROJ)[0] * CHUNKS + (c + 1))
                    cols = src[:, c, :, 0:FIELDS]
                    wait(pe, q_ready, n)
                    pe.matmul(q_ps[:, 0:COLS], w_att[:, l, 0, :], cols, start=True, stop=True).then_inc(q_done, 1)
                    wait(pe, k_ready, n)
                    pe.matmul(k_ps[:, 0:COLS], w_att[:, l, 1, :], cols, start=True, stop=True).then_inc(k_done, 1)
                    wait(pe, v_ready, n)
                    for g in range(QUADS):
                        last = pe.matmul(v_ps[:, g * PE_ROWS:(g + 1) * PE_ROWS], src[:, c, 4 * g:4 * g + 4, :],
                                         w_att[:, l, 2, :], start=True, stop=True)
                    last.then_inc(v_done, 1)

                u, n, there = unit(it, s + SCORE)
                if there:
                    wait(pe, q_ready, n + 1)
                    wait(pe, k_ready, n + 1)
                    wait(pe, sub_done, n)
                    for p in range(CHUNK):
                        g, a = divmod(p, 4)
                        last = pe.matmul(s_ps[FP * a:FP * a + FP, g * QCOLS:(g + 1) * QCOLS], q_sb[u % 2][:, p, :],
                                         k_bd[u % 2][:, p, :, :], start=True, stop=True)
                    last.then_inc(s_done, 1)

                u, n, there = unit(it, s)
                if there:
                    l, c = divmod(u, CHUNKS)
                    src = x if l else x0
                    wait(pe, x_ready, n)
                    pe.matmul(o_ps[:, 0:COLS], w_att[:, l, 3, :], src[:, c, :, 0:FIELDS], start=True, stop=False,
                              skip_group_check=True)
                    wait(pe, v_ready, n + 1)
                    wait(pe, pt_ready, n + 1)
                    for g in range(QUADS):
                        for b in range(BLOCKS):
                            last = pe.matmul(o_ps[FP * b:FP * b + FP, g * QCOLS:(g + 1) * QCOLS],
                                             v_sb[u % VSLOTS][:, g, HD * b:HD * b + HD],
                                             pt_bd[u % 2][:, g * BLOCKS + b, :, 0:FIELDS], start=False, stop=True,
                                             skip_group_check=True)
                    last.then_inc(o_done, 1)

                i, there = turn(it, s)
                if there and u < 2 * DNN_SLOTS:
                    half, part = divmod(u, DNN_SLOTS)
                    hidden = slice(half * PE_ROWS, (half + 1) * PE_ROWS)
                    if u == 0:
                        wait(pe, h1_ready, i)
                        wait(pe, x0_ready, i * CHUNKS + CHUNKS)
                        wait(pe, x_den_loaded, (i + 1) * 32)
                    if part == 0:
                        for e in range(2):
                            pe.matmul(d_ps[e][:, half * PAIRS:(half + 1) * PAIRS], w1_den[EMB * e:EMB * e + DENSE, hidden],
                                      x_den[EMB * e:EMB * e + DENSE, :], start=True, stop=False)
                    for f in range(part * FIELDS_PER_SLOT, min((part + 1) * FIELDS_PER_SLOT, FIELDS)):
                        for e in range(2):
                            rows_e = slice(EMB * e, EMB * e + EMB)
                            last = pe.matmul(d_ps[e][:, half * PAIRS:(half + 1) * PAIRS], w1_emb[rows_e, f, hidden],
                                             x0[rows_e, :, :, f].rearrange("p c n -> p (c n)"), start=False, stop=f == FIELDS - 1)
                    if u == 2 * DNN_SLOTS - 1:
                        last.then_inc(dnn_done, 1)

                if there and u == L2_SLOT:
                    wait(pe, h1_ready, i + 1)
                    wait(pe, x0_ready, i * CHUNKS + CHUNKS)
                    wait(pe, logit_ready, i)
                    for k in range(2):
                        last = pe.matmul(t_ps[:, 0:EXAMPLES], w2_sb[:, k, :], h1[:, k, :, :], start=k == 0, stop=k == 1)
                    last.then_inc(l2_done, 1)

                i, there = turn(it, s, back=-1)
                if there and X0_SLOT <= u < X0_SLOT + CHUNKS:
                    if u == X0_SLOT:
                        wait(pe, h2_ready, i)
                    embed(i, u - X0_SLOT)

                i, there = turn(it, s, back=1)
                if there and u == FINAL_SLOT:
                    wait(pe, x_all_loaded, (i + 1) * 16)
                    wait(pe, att_done, (i + 1) * CHUNKS)
                    wait(pe, h2_ready, i + 1)
                    if not isinstance(i, int) or i + 1 < ITERATIONS:
                        wait(pe, x0_ready, i * CHUNKS + 2 * CHUNKS)
                    pe.matmul(t_ps[0:2, PAIRS:2 * PAIRS], pick[:, :], att_part[:, :], start=True, stop=False)
                    for e in range(2):
                        pe.matmul(t_ps[0:2, PAIRS:2 * PAIRS], ow_dnn_sb[:, e, :], h2[:, e, :], start=False, stop=e == 1)
                    for e in range(2):
                        last = pe.matmul(t_ps[0:2, 0:PAIRS], lw_sb[:, e, :], x_all[:, e, :], start=e == 0, stop=e == 1)
                    last.then_inc(final_done, 1)

            over_slots(pe, slot)

        @block.scalar
        def _(act):
            def embed(it, c):
                wait(act, xt_done, it * CHUNKS + (c + 1))
                act.activation(x0[:, c, :, 0:FIELDS], t_ps[:, 0:COLS].rearrange("p (n f) -> p n f", f=FIELDS),
                               ACT.Copy).then_inc(x0_ready, 1)

            act.wait_ge(buf_zeroed, 2)
            for c in range(CHUNKS):
                embed(0, c)
            act.wait_ge(buf_zeroed, 10)
            act.wait_ge(dnn_w_loaded, 16 * 15)

            def slot(it, s):
                u, n, there = unit(it, s + PROJ)
                if there:
                    wait(act, q_done, n + 1)
                    wait(act, s_done, n - 1)
                    act.activation(q_sb[u % 2][:, :, 0:FIELDS], q_ps[:, 0:COLS].rearrange("p (n f) -> p n f", f=FIELDS),
                                   ACT.Copy).then_inc(q_ready, 1)
                    wait(act, k_done, n + 1)
                    for b in range(BLOCKS):
                        part = slice(FP * b, FP * b + FP)
                        last = act.activation(k_bd[u % 2][part, :, b, :],
                                              k_ps[part, 0:COLS].rearrange("p (n f) -> p n f", f=FIELDS), ACT.Copy)
                    last.then_inc(k_ready, 1)
                    wait(act, v_done, n + 1)
                    wait(act, o_done, n + (1 - VSLOTS))
                    act.activation(v_sb[u % VSLOTS][:, :, :].rearrange("p g n -> p (g n)"), v_ps[:, :], ACT.Copy).then_inc(v_ready, 1)

                u, n, there = unit(it, s + SCORE)
                if there:
                    wait(act, sub_done, n + 1)
                    act.activation(e_sb[u % 2][:, :, :], e_sb[u % 2][:, :, :], ACT.Exp).then_inc(exp_done, 1)

                u, n, there = unit(it, s)
                if there:
                    c = u % CHUNKS
                    wait(act, o_done, n + 1)
                    if u < CHUNKS:
                        wait(act, att_done, turn(it, s)[0] * CHUNKS)
                    act.activation(x[:, c, :, 0:FIELDS], o_ps[:, 0:COLS].rearrange("p (n f) -> p n f", f=FIELDS),
                                   ACT.Relu).then_inc(x_ready, 1)

                i, there = turn(it, s)
                if there and u == H1_SLOT:
                    wait(act, dnn_done, i + 1)
                    for half in range(2):
                        for e in range(2):
                            last = act.activation(h1[:, half, e, :], d_ps[e][:, half * PAIRS:(half + 1) * PAIRS], ACT.Relu,
                                                  bias=b1_sb[:, half:half + 1])
                    last.then_inc(h1_ready, 1)
                if there and u == L2_SLOT:
                    wait(act, l2_done, i + 1)
                    act.activation(h2[:, :, :].rearrange("p e n -> p (e n)"), t_ps[:, 0:EXAMPLES], ACT.Relu,
                                   bias=b2_sb[:, 0:1]).then_inc(h2_ready, 1)

                i, there = turn(it, s, back=-1)
                if there and X0_SLOT <= u < X0_SLOT + CHUNKS:
                    embed(i, u - X0_SLOT)

                i, there = turn(it, s, back=1)
                if there and u == FINAL_SLOT:
                    wait(act, final_done, i + 1)
                    act.activation(lin[:, :], t_ps[0:2, 0:PAIRS], ACT.Relu, bias=lb_sb[:, 0:1]).then_inc(lin_ready, 1)
                if there and u == SUM_SLOT:
                    wait(act, logit_ready, i + 1)
                    act.activation(expneg[:, :], logit[:, :], ACT.Exp, scale=-1.0).then_inc(expneg_ready, 1)

            over_slots(act, slot)

        @block.vector
        def _(dve):
            for t in (x0, x):
                dve.memset(t[:, :, :, :], 0.0).then_inc(buf_zeroed, 1)
            for t in q_sb:
                dve.memset(t[:, :, :], 0.0).then_inc(buf_zeroed, 1)
            for t in k_bd:
                dve.memset(t[:, :, :, :], 0.0).then_inc(buf_zeroed, 1)
            dve.memset(p_sb[:, :, :], 0.0).then_inc(buf_zeroed, 1)
            for t in pt_bd:
                dve.memset(t[:, :, :, :], 0.0).then_inc(buf_zeroed, 1)
            dve.memset(pick[:, :], 0.0).then_inc(buf_zeroed, 1)
            dve.wait_ge(buf_zeroed, 10)
            for e in range(2):
                dve.memset(pick[EMB * e:EMB * e + EMB, e:e + 1], 1.0).then_inc(buf_zeroed, 1)
            dve.wait_ge(dnn_w_loaded, 16 * 15)

            def transpose(u, a):
                part = slice(FP * a, FP * a + FP)
                return dve.transpose(pt_bd[u % 2][part, :, a, :], p_sb[part, :, :])

            def slot(it, s):
                u1, n1, there1 = unit(it, s + SCORE)
                u2, n2, there2 = unit(it, s + SCORE - 1)
                wide = [PE_ROWS, QUADS * BLOCKS, FIELDS]
                scores = s_ps[:, 0:COLS].rearrange("p (m k) -> p m k", k=FIELDS)
                if there1:
                    wait(dve, s_done, n1 + 1)
                    dve.tensor_reduce(row_max[:, :], scores, AX, ALU.max).then_inc(max_done, 1)
                if there2:
                    wait(dve, p_ready, n2 + 1)
                    wait(dve, o_done, n2 - 1)
                    transpose(u2, 0)
                if there1:
                    wait(dve, max_done, n1 + 1)
                    dve.tensor_tensor(e_sb[u1 % 2][:, :, :], scores, row_max[:, :].unsqueeze(2).to_broadcast(wide),
                                      ALU.subtract).then_inc(sub_done, 1)
                if there2:
                    for a in range(1, 4):
                        last = transpose(u2, a)
                    last.then_inc(pt_ready, 1)
                if there1:
                    e = e_sb[u1 % 2]
                    wait(dve, exp_done, n1 + 1)
                    dve.tensor_reduce(row_sum[:, :], e[:, :, :], AX, ALU.add).then_inc(sum_done, 1)
                    wait(dve, sum_done, n1 + 1)
                    dve.reciprocal(row_inv[:, :], row_sum[:, :]).then_inc(inv_done, 1)
                    wait(dve, inv_done, n1 + 1)
                    wait(dve, pt_ready, n1)
                    dve.tensor_tensor(p_sb[:, :, 0:FIELDS], e[:, :, :], row_inv[:, :].unsqueeze(2).to_broadcast(wide),
                                      ALU.mult).then_inc(p_ready, 1)

                u, n, there = unit(it, s - 1)
                if there and u >= (LAYERS - 1) * CHUNKS:
                    c = u % CHUNKS
                    count = turn(it, s - 1)[0] * CHUNKS + (c + 1)
                    wait(dve, x_ready, n + 1)
                    wait(dve, att_done, count - 1)
                    dve.tensor_tensor(weighed[:, :, :], x[:, c, :, 0:FIELDS],
                                      ow_att_sb[:, :].unsqueeze(1).to_broadcast([PE_ROWS, CHUNK, FIELDS]),
                                      ALU.mult).then_inc(weighed_done, 1)
                    wait(dve, weighed_done, count)
                    if c == 0:
                        wait(dve, final_done, turn(it, s - 1)[0])
                    dve.tensor_reduce(att_part[:, c * CHUNK:(c + 1) * CHUNK], weighed[:, :, :], AX, ALU.add).then_inc(att_done, 1)

                i, there = turn(it, s, back=1)
                if there and s % UNITS == SUM_SLOT:
                    wait(dve, lin_ready, i + 1)
                    dve.tensor_tensor(logit[:, :], t_ps[0:2, PAIRS:2 * PAIRS], lin[:, :], ALU.add).then_inc(logit_ready, 1)
                if there and s % UNITS == SIGMOID_SLOT:
                    wait(dve, expneg_ready, i + 1)
                    dve.tensor_scalar(denom[:, :], expneg[:, :], 1.0, None, ALU.add).then_inc(denom_ready, 1)
                    wait(dve, denom_ready, i + 1)
                    wait(dve, stored, i * 16)
                    dve.reciprocal(result[:, :], denom[:, :]).then_inc(result_ready, 1)

            over_slots(dve, slot)


_NAMES = ["table", "idx", "offs", "xt", "wq", "wk", "wv", "wr", "w1", "b1", "w2", "b2", "ow_att", "ow_dnn", "lw", "lb"]


def kernel(**inputs):
    import concourse.bacc as _bacc
    from concourse.bass_utils import run_bass_kernel_spmd as _run

    g = {k.replace("L0_rec_", ""): np.asarray(v) for k, v in inputs.items()}
    idx = g["r_sparse_idx"].reshape(ITERATIONS, 2, PAIRS // 4, 4, FIELDS)
    att = FIELDS * EMB
    laid = {
        "table": g["emb_tables"].reshape(FIELDS * VOCAB, EMB),
        "idx": idx.transpose(3, 4, 0, 2, 1).reshape(QCOLS, ITERATIONS, PAIRS // 4 * 2),
        "offs": np.tile(np.arange(FIELDS, dtype=np.int32) * VOCAB, 4).reshape(QCOLS, 1),
        "xt": g["r_X"].reshape(ITERATIONS, 2, PAIRS, FEATURES).transpose(0, 3, 1, 2),
        "wq": g["Wq"], "wk": g["Wk"], "wv": g["Wv"], "wr": g["Wres"],
        "w1": g["dnn_W1"], "b1": g["dnn_b1"].reshape(2, PE_ROWS).T,
        "w2": g["dnn_W2"], "b2": g["dnn_b2"].reshape(HIDDEN2, 1),
        "ow_att": g["out_W"][:att].reshape(FIELDS, EMB).T, "ow_dnn": g["out_W"][att:],
        "lw": g["lin_W"], "lb": g["lin_b"].reshape(1, 1),
    }
    nc = _bacc.Bacc("TRN2", target_bir_lowering=False, num_devices=1)
    arrays, args = {}, []
    for name in _NAMES:
        a = np.ascontiguousarray(laid[name])
        arrays[f"in_{name}"] = a
        args.append(nc.dram_tensor(f"in_{name}", a.shape, mybir.dt.from_np(a.dtype), kind="ExternalInput").ap())
    out = nc.dram_tensor("out", (ITERATIONS, 2, PAIRS), mybir.dt.float32, kind="ExternalOutput").ap()
    interacting_attention_recommender(nc, *args, out)
    r = _run(nc, [arrays], core_ids=[0])
    return np.asarray(r.results[0]["out"]).reshape(BATCH, 1)
```

```python
import numpy as np
import concourse.bass as bass
from concourse import mybir
from contextlib import ExitStack

BATCH, FIELDS, DENSE, VOCAB, EMB = 16384, 26, 13, 10000, 64
HEADS, LAYERS, HIDDEN1, HIDDEN2 = 2, 3, 256, 128
FEATURES = FIELDS + DENSE
HD = EMB // HEADS
PE_ROWS = 128
FP = 32
PAIRS = 128
EXAMPLES = 2 * PAIRS
ITERATIONS = BATCH // EXAMPLES
CHUNK = 16
CHUNKS = PAIRS // CHUNK
QUADS = CHUNK // 4
BLOCKS = 4
COLS = CHUNK * FIELDS
QCOLS = 4 * FIELDS
UNITS = LAYERS * CHUNKS
PROJ, SCORE = 3, 2
TURN = CHUNKS - PROJ
VSLOTS = 4
TWINS = FIELDS // 2
PRODUCTS = 2 * (TWINS + 1)
DNN_SLOT, PER_SLOT = TURN, 4
H1_SLOT = DNN_SLOT + -(-PRODUCTS // PER_SLOT) - 1
L2_SLOT, X0_SLOT = H1_SLOT + 1, H1_SLOT + 2
FINAL_SLOT, SUM_SLOT, SIGMOID_SLOT = 1, 2, 3


def interacting_attention_recommender(nc, table, idx, offs, xt, wq, wk, wv, wr, w1, b1, w2, b2,
                                      ow_att, ow_dnn, lw, lb, out):
    fp32, i32 = mybir.dt.float32, mybir.dt.int32
    ALU = mybir.AluOpType
    ACT = mybir.ActivationFunctionType
    AX = mybir.AxisListType.X

    ctx = ExitStack()
    with ctx:
        def sb(name, shape, dt=fp32):
            return ctx.enter_context(nc.sbuf_tensor(name, shape, dt))

        def bank(name):
            return ctx.enter_context(nc.psum_tensor(name, [PE_ROWS, 512], fp32))

        def sem(name):
            return ctx.enter_context(nc.semaphore(name))

        w_att = sb("w_att", [PE_ROWS, LAYERS, 4, PE_ROWS])
        w1_emb = sb("w1_emb", [PE_ROWS, TWINS, HIDDEN1])
        w1_den = sb("w1_den", [DENSE, HIDDEN1])
        w2_sb = sb("w2_sb", [PE_ROWS, 2, HIDDEN2])
        b1_sb = sb("b1_sb", [PE_ROWS, 2])
        b2_sb = sb("b2_sb", [PE_ROWS, 1])
        ow_att_sb = sb("ow_att_sb", [PE_ROWS, FIELDS])
        ow_dnn_sb = sb("ow_dnn_sb", [PE_ROWS, 2, 2])
        lw_sb = sb("lw_sb", [FEATURES, 2, 2])
        lb_sb = sb("lb_sb", [2, 1])
        pick = sb("pick", [PE_ROWS, 2])
        ident = sb("ident", [PE_ROWS, PE_ROWS])
        idx_all = sb("idx_all", [QCOLS, ITERATIONS, PAIRS // 4 * 2], i32)
        offs_sb = sb("offs_sb", [QCOLS, 1], i32)
        idx_now = sb("idx_now", [QCOLS, PAIRS // 4 * 2], i32)
        rows = sb("rows", [QCOLS, PAIRS // 4, PE_ROWS])
        x0 = sb("x0", [PE_ROWS, CHUNKS, CHUNK, FP])
        x_dnn = sb("x_dnn", [PE_ROWS, TWINS, 2, CHUNKS, CHUNK])
        x = sb("x", [PE_ROWS, CHUNKS, CHUNK, FP])
        q_sb = [sb(f"q_sb{i}", [PE_ROWS, CHUNK, FP]) for i in range(2)]
        k_bd = [sb(f"k_bd{i}", [PE_ROWS, CHUNK, BLOCKS, FIELDS]) for i in range(2)]
        v_sb = [sb(f"v_sb{i}", [PE_ROWS, QUADS, PE_ROWS]) for i in range(VSLOTS)]
        e_sb = [sb(f"e_sb{i}", [PE_ROWS, QUADS * BLOCKS, FIELDS]) for i in range(2)]
        pt_sb = sb("pt_sb", [PE_ROWS, QUADS * BLOCKS, FP])
        p_sb = sb("p_sb", [PE_ROWS, QUADS * BLOCKS, FP])
        pt_bd = [sb(f"pt_bd{i}", [PE_ROWS, QUADS * BLOCKS, 4, FP]) for i in range(2)]
        row_max = sb("row_max", [PE_ROWS, QUADS * BLOCKS])
        row_sum = sb("row_sum", [PE_ROWS, QUADS * BLOCKS])
        row_inv = sb("row_inv", [PE_ROWS, QUADS * BLOCKS])
        weighed = sb("weighed", [PE_ROWS, CHUNK, FIELDS])
        att_part = sb("att_part", [PE_ROWS, PAIRS])
        x_den = sb("x_den", [DENSE, 2, PAIRS])
        x_all = sb("x_all", [FEATURES, 2, PAIRS])
        h1 = sb("h1", [PE_ROWS, 2, 2, PAIRS])
        h2 = sb("h2", [PE_ROWS, 2, PAIRS])
        lin = sb("lin", [2, PAIRS])
        logit = sb("logit", [2, PAIRS])
        expneg = sb("expneg", [2, PAIRS])
        denom = sb("denom", [2, PAIRS])
        result = sb("result", [2, PAIRS])

        q_ps, k_ps, v_ps, s_ps, o_ps, t_ps = (bank(n) for n in ("q_ps", "k_ps", "v_ps", "s_ps", "o_ps", "t_ps"))
        d_ps = [bank("d_ps0"), bank("d_ps1")]

        w_zeroed = sem("w_zeroed")
        buf_zeroed = sem("buf_zeroed")
        ident_ready = sem("ident_ready")
        att_w_loaded = sem("att_w_loaded")
        dnn_w_loaded = sem("dnn_w_loaded")
        idx_loaded = sem("idx_loaded")
        idx_ready = sem("idx_ready")
        gathered = [sem(f"gathered{c}") for c in range(CHUNKS)]
        x_den_loaded = sem("x_den_loaded")
        x_all_loaded = sem("x_all_loaded")
        xt_done = sem("xt_done")
        x0_ready = sem("x0_ready")
        q_done, k_done, v_done = sem("q_done"), sem("k_done"), sem("v_done")
        q_ready, k_ready, v_ready = sem("q_ready"), sem("k_ready"), sem("v_ready")
        s_done = sem("s_done")
        max_done, sub_done = sem("max_done"), sem("sub_done")
        exp_done = sem("exp_done")
        sum_done, inv_done, p_ready = sem("sum_done"), sem("inv_done"), sem("p_ready")
        pt_done = sem("pt_done")
        pt_ready = sem("pt_ready")
        o_done = sem("o_done")
        x_ready = sem("x_ready")
        weighed_done, att_done = sem("weighed_done"), sem("att_done")
        dnn_done = sem("dnn_done")
        h1_ready = sem("h1_ready")
        l2_done = sem("l2_done")
        h2_ready = sem("h2_ready")
        final_done = sem("final_done")
        lin_ready, logit_ready, expneg_ready = sem("lin_ready"), sem("logit_ready"), sem("expneg_ready")
        denom_ready, result_ready = sem("denom_ready"), sem("result_ready")
        stored = sem("stored")
        cleared, sp_cleared = sem("cleared"), sem("sp_cleared")

        def unit(it, s):
            n = it * UNITS + s
            return s % UNITS, n, not isinstance(n, int) or 0 <= n < ITERATIONS * UNITS

        def turn(it, s, back=0):
            i = it + (s // UNITS - back)
            return i, not isinstance(i, int) or 0 <= i < ITERATIONS

        def wait(eng, semaphore, value):
            if not isinstance(value, int) or value > 0:
                eng.wait_ge(semaphore, value)

        def over_slots(eng, slot):
            for s in range(-PROJ, TURN):
                slot(0, s)
            with eng.Fori(0, ITERATIONS - 1) as it:
                for s in range(TURN, TURN + UNITS):
                    slot(it, s)
            for s in range(TURN, TURN + UNITS):
                slot(ITERATIONS - 1, s)

        DNN_LOADS = 16 * 14

        block = ctx.enter_context(nc.Block())

        @block.sync
        def _(sp):
            sp.dma_start(idx_all[:, :, :], idx).then_inc(idx_loaded, 16)
            sp.dma_start(offs_sb[:, :], offs).then_inc(idx_loaded, 16)
            sp.wait_ge(w_zeroed, 3)
            for kind, w in enumerate((wq, wk, wv, wr)):
                for e in range(2):
                    half = slice(EMB * e, EMB * e + EMB)
                    sp.dma_start(w_att[half, :, kind, half], w.rearrange("l f o -> f l o")).then_inc(att_w_loaded, 16)
            for e in range(2):
                half = slice(EMB * e, EMB * e + EMB)
                sp.dma_start(w1_emb[half, :, :], w1[DENSE:, :].rearrange("(i t f) o -> t f i o", t=2, f=EMB)[e]).then_inc(dnn_w_loaded, 16)
                sp.dma_start(ow_att_sb[half, :], ow_att).then_inc(dnn_w_loaded, 16)
                sp.dma_start(ow_dnn_sb[:, e, e:e + 1], ow_dnn).then_inc(dnn_w_loaded, 16)
                sp.dma_start(lw_sb[:, e, e:e + 1], lw).then_inc(dnn_w_loaded, 16)
                sp.dma_start(lb_sb[e:e + 1, :], lb).then_inc(dnn_w_loaded, 16)
            sp.dma_start(w1_den[:, :], w1[0:DENSE, :]).then_inc(dnn_w_loaded, 16)
            sp.dma_start(x_den[:, :, :], xt[0, FIELDS:, :, :]).then_inc(x_den_loaded, 16)
            sp.dma_start(w2_sb[:, :, :], w2.rearrange("(k p) o -> p k o", p=PE_ROWS)).then_inc(dnn_w_loaded, 16)
            sp.dma_start(b1_sb[:, :], b1).then_inc(dnn_w_loaded, 16)
            sp.dma_start(b2_sb[:, :], b2).then_inc(dnn_w_loaded, 16)
            sp.dma_start(x_all[:, :, :], xt[0]).then_inc(x_all_loaded, 16)

            def store(it):
                sp.wait_ge(result_ready, it + 1)
                sp.sem_inc(sp_cleared, 1)
                sp.dma_start(out[it], result[:, :]).then_inc(stored, 16)

            with sp.Fori(0, ITERATIONS - 1) as it:
                sp.wait_ge(dnn_done, it + 1)
                sp.sem_inc(sp_cleared, 1)
                sp.dma_start(x_den[:, :, :], xt[it + 1, FIELDS:, :, :]).then_inc(x_den_loaded, 16)
                sp.wait_ge(final_done, it + 1)
                sp.sem_inc(sp_cleared, 1)
                sp.dma_start(x_all[:, :, :], xt[it + 1]).then_inc(x_all_loaded, 16)
                store(it)
            store(ITERATIONS - 1)
            sp.wait_ge(stored, 16 * ITERATIONS)

        @block.gpsimd
        def _(pool):
            pool.memset(w_att[:, :, :, :], 0.0).then_inc(w_zeroed, 1)
            pool.memset(ow_dnn_sb[:, :, :], 0.0).then_inc(w_zeroed, 1)
            pool.memset(lw_sb[:, :, :], 0.0).then_inc(w_zeroed, 1)
            pool.memset(ident[:, :], 0.0).then_inc(ident_ready, 1)
            pool.wait_ge(ident_ready, 1)
            pool.affine_select(out=ident[:, :], in_=ident[:, :], compare_op=ALU.not_equal, fill=1.0,
                               base=0, pattern=[[-1, PE_ROWS]], channel_multiplier=1).then_inc(ident_ready, 1)
            pool.wait_ge(idx_loaded, 32)

            def gather(it, first):
                if not first:
                    for c in range(CHUNKS):
                        pool.wait_ge(gathered[c], it * (16 * 2 * QUADS))
                pool.tensor_tensor(idx_now[:, :], idx_all[:, it, :], offs_sb[:, :].to_broadcast([QCOLS, PAIRS // 4 * 2]),
                                   ALU.add).then_inc(idx_ready, 1)
                pool.wait_ge(idx_ready, it + 1)
                pool.sem_inc(cleared, 1)
                for c in range(CHUNKS):
                    if not first:
                        pool.wait_ge(xt_done, it * CHUNKS + (c + 1 - CHUNKS))
                    pool.sem_inc(cleared, 1)
                    for g in range(c * QUADS, (c + 1) * QUADS):
                        for e in range(2):
                            pool.indirect_dma_start(
                                out=rows[:, g, EMB * e:EMB * e + EMB], out_offset=None, in_=table,
                                in_offset=bass.IndirectOffsetOnAxis(ap=idx_now[:, 2 * g + e:2 * g + e + 1], axis=0),
                            ).then_inc(gathered[c], 16)

            gather(0, True)
            with pool.Fori(1, ITERATIONS) as it:
                gather(it, False)

        @block.tensor
        def _(pe):
            def embed(it, c):
                wait(pe, gathered[c], (it + 1) * (16 * 2 * QUADS))
                wait(pe, x0_ready, it * CHUNKS + c)
                for g in range(QUADS):
                    last = pe.transpose(t_ps[:, g * QCOLS:(g + 1) * QCOLS], rows[:, c * QUADS + g, :], ident[0:QCOLS, 0:QCOLS])
                last.then_inc(xt_done, 1)

            pe.wait_ge(ident_ready, 2)
            pe.wait_ge(att_w_loaded, 16 * 8)

            def slot(it, s):
                if s < TURN:
                    embed(0, s + PROJ)
                u, n, there = unit(it, s + PROJ)
                if there:
                    l, c = divmod(u, CHUNKS)
                    src = x if l else x0
                    if l:
                        wait(pe, x_ready, n + (1 - CHUNKS))
                    else:
                        wait(pe, x0_ready, turn(it, s + PROJ)[0] * CHUNKS + (c + 1))
                    cols = src[:, c, :, 0:FIELDS]
                    wait(pe, q_ready, n)
                    pe.matmul(q_ps[:, 0:COLS], w_att[:, l, 0, :], cols, start=True, stop=True).then_inc(q_done, 1)
                    wait(pe, k_ready, n)
                    pe.matmul(k_ps[:, 0:COLS], w_att[:, l, 1, :], cols, start=True, stop=True).then_inc(k_done, 1)
                    wait(pe, v_ready, n)
                    for g in range(QUADS):
                        last = pe.matmul(v_ps[:, g * PE_ROWS:(g + 1) * PE_ROWS], src[:, c, 4 * g:4 * g + 4, :],
                                         w_att[:, l, 2, :], start=True, stop=True)
                    last.then_inc(v_done, 1)

                u, n, there = unit(it, s + SCORE)
                if there:
                    wait(pe, q_ready, n + 1)
                    wait(pe, k_ready, n + 1)
                    wait(pe, sub_done, n)
                    for p in range(CHUNK):
                        g, a = divmod(p, 4)
                        last = pe.matmul(s_ps[FP * a:FP * a + FP, g * QCOLS:(g + 1) * QCOLS], q_sb[u % 2][:, p, :],
                                         k_bd[u % 2][:, p, :, :], start=True, stop=True)
                    last.then_inc(s_done, 1)

                u, n, there = unit(it, s)
                if there:
                    l, c = divmod(u, CHUNKS)
                    src = x if l else x0
                    wait(pe, x_ready, n)
                    pe.matmul(o_ps[:, 0:COLS], w_att[:, l, 3, :], src[:, c, :, 0:FIELDS], start=True, stop=False,
                              skip_group_check=True)
                    wait(pe, v_ready, n + 1)
                    wait(pe, pt_ready, n + 1)
                    for g in range(QUADS):
                        for b in range(BLOCKS):
                            last = pe.matmul(o_ps[FP * b:FP * b + FP, g * QCOLS:(g + 1) * QCOLS],
                                             v_sb[u % VSLOTS][:, g, HD * b:HD * b + HD],
                                             pt_bd[u % 2][:, g * BLOCKS + b, :, 0:FIELDS], start=False, stop=True,
                                             skip_group_check=True)
                    last.then_inc(o_done, 1)

                i, there = turn(it, s)
                if there and DNN_SLOT <= u <= H1_SLOT:
                    if u == DNN_SLOT:
                        pe.wait_ge(dnn_w_loaded, DNN_LOADS)
                        wait(pe, h1_ready, i)
                        wait(pe, x0_ready, i * CHUNKS + CHUNKS)
                        wait(pe, x_den_loaded, (i + 1) * 16)
                    done = (u - DNN_SLOT) * PER_SLOT
                    for product in range(done, min(done + PER_SLOT, PRODUCTS)):
                        half, t = divmod(product, TWINS + 1)
                        hidden = slice(half * PE_ROWS, (half + 1) * PE_ROWS)
                        if t < TWINS:
                            last = pe.matmul(d_ps[half][:, 0:EXAMPLES], w1_emb[:, t, hidden],
                                             x_dnn[:, t, :, :, :].rearrange("p e c n -> p (e c n)"), start=t == 0, stop=False)
                        else:
                            last = pe.matmul(d_ps[half][:, 0:EXAMPLES], w1_den[:, hidden],
                                             x_den[:, :, :].rearrange("p e n -> p (e n)"), start=False, stop=True)
                    if u == H1_SLOT:
                        last.then_inc(dnn_done, 1)

                if there and u == L2_SLOT:
                    wait(pe, h1_ready, i + 1)
                    wait(pe, logit_ready, i)
                    for k in range(2):
                        last = pe.matmul(t_ps[:, 0:EXAMPLES], w2_sb[:, k, :], h1[:, k, :, :], start=k == 0, stop=k == 1)
                    last.then_inc(l2_done, 1)

                i, there = turn(it, s, back=-1)
                if there and X0_SLOT <= u < X0_SLOT + CHUNKS:
                    if u == X0_SLOT:
                        wait(pe, h2_ready, i)
                    embed(i, u - X0_SLOT)

                i, there = turn(it, s, back=1)
                if there and u == FINAL_SLOT:
                    wait(pe, x_all_loaded, (i + 1) * 16)
                    wait(pe, att_done, (i + 1) * CHUNKS)
                    wait(pe, h2_ready, i + 1)
                    if not isinstance(i, int) or i + 1 < ITERATIONS:
                        wait(pe, x0_ready, i * CHUNKS + 2 * CHUNKS)
                    pe.matmul(t_ps[0:2, PAIRS:2 * PAIRS], pick[:, :], att_part[:, :], start=True, stop=False)
                    for e in range(2):
                        pe.matmul(t_ps[0:2, PAIRS:2 * PAIRS], ow_dnn_sb[:, e, :], h2[:, e, :], start=False, stop=e == 1)
                    for e in range(2):
                        last = pe.matmul(t_ps[0:2, 0:PAIRS], lw_sb[:, e, :], x_all[:, e, :], start=e == 0, stop=e == 1)
                    last.then_inc(final_done, 1)

            over_slots(pe, slot)

        @block.scalar
        def _(act):
            def embed(it, c):
                wait(act, xt_done, it * CHUNKS + (c + 1))
                twins = t_ps[:, 0:COLS].rearrange("p (n i t) -> p t i n", t=2, i=TWINS)
                for e in range(2):
                    for t in range(2):
                        act.activation(x_dnn[EMB * t:EMB * t + EMB, :, e, c, :], twins[EMB * e:EMB * e + EMB, t, :, :], ACT.Copy)
                act.activation(x0[:, c, :, 0:FIELDS], t_ps[:, 0:COLS].rearrange("p (n f) -> p n f", f=FIELDS),
                               ACT.Copy).then_inc(x0_ready, 1)

            act.wait_ge(buf_zeroed, 5)

            def slot(it, s):
                if s < TURN:
                    embed(0, s + PROJ)
                u, n, there = unit(it, s + PROJ)
                if there:
                    wait(act, q_done, n + 1)
                    wait(act, s_done, n - 1)
                    act.activation(q_sb[u % 2][:, :, 0:FIELDS], q_ps[:, 0:COLS].rearrange("p (n f) -> p n f", f=FIELDS),
                                   ACT.Copy).then_inc(q_ready, 1)
                    wait(act, k_done, n + 1)
                    for b in range(BLOCKS):
                        part = slice(FP * b, FP * b + FP)
                        last = act.activation(k_bd[u % 2][part, :, b, :],
                                              k_ps[part, 0:COLS].rearrange("p (n f) -> p n f", f=FIELDS), ACT.Copy)
                    last.then_inc(k_ready, 1)
                    wait(act, v_done, n + 1)
                    wait(act, o_done, n + (1 - VSLOTS))
                    act.activation(v_sb[u % VSLOTS][:, :, :].rearrange("p g n -> p (g n)"), v_ps[:, :], ACT.Copy).then_inc(v_ready, 1)

                u, n, there = unit(it, s + SCORE)
                if there:
                    wait(act, sub_done, n + 1)
                    act.activation(e_sb[u % 2][:, :, :], e_sb[u % 2][:, :, :], ACT.Exp).then_inc(exp_done, 1)

                u, n, there = unit(it, s)
                if there:
                    c = u % CHUNKS
                    act.wait_ge(buf_zeroed, 10)
                    wait(act, o_done, n + 1)
                    if u < CHUNKS:
                        wait(act, att_done, turn(it, s)[0] * CHUNKS)
                    act.activation(x[:, c, :, 0:FIELDS], o_ps[:, 0:COLS].rearrange("p (n f) -> p n f", f=FIELDS),
                                   ACT.Relu).then_inc(x_ready, 1)

                i, there = turn(it, s)
                if there and u == H1_SLOT:
                    wait(act, dnn_done, i + 1)
                    act.wait_ge(dnn_w_loaded, DNN_LOADS)
                    for half in range(2):
                        last = act.activation(h1[:, half, :, :].rearrange("p e n -> p (e n)"), d_ps[half][:, 0:EXAMPLES],
                                              ACT.Relu, bias=b1_sb[:, half:half + 1])
                    last.then_inc(h1_ready, 1)
                if there and u == L2_SLOT:
                    wait(act, l2_done, i + 1)
                    act.activation(h2[:, :, :].rearrange("p e n -> p (e n)"), t_ps[:, 0:EXAMPLES], ACT.Relu,
                                   bias=b2_sb[:, 0:1]).then_inc(h2_ready, 1)

                i, there = turn(it, s, back=-1)
                if there and X0_SLOT <= u < X0_SLOT + CHUNKS:
                    embed(i, u - X0_SLOT)

                i, there = turn(it, s, back=1)
                if there and u == FINAL_SLOT:
                    wait(act, final_done, i + 1)
                    act.activation(lin[:, :], t_ps[0:2, 0:PAIRS], ACT.Relu, bias=lb_sb[:, 0:1]).then_inc(lin_ready, 1)
                if there and u == SUM_SLOT:
                    wait(act, logit_ready, i + 1)
                    act.activation(expneg[:, :], logit[:, :], ACT.Exp, scale=-1.0).then_inc(expneg_ready, 1)

            over_slots(act, slot)

        @block.vector
        def _(dve):
            dve.memset(x0[:, :, :, :], 0.0).then_inc(buf_zeroed, 1)
            for t in q_sb:
                dve.memset(t[:, :, :], 0.0).then_inc(buf_zeroed, 1)
            for t in k_bd:
                dve.memset(t[:, :, :, :], 0.0).then_inc(buf_zeroed, 1)
            dve.memset(x[:, :, :, :], 0.0).then_inc(buf_zeroed, 1)
            dve.memset(p_sb[:, :, :], 0.0).then_inc(buf_zeroed, 1)
            for t in pt_bd:
                dve.memset(t[:, :, :, :], 0.0).then_inc(buf_zeroed, 1)
            dve.memset(pick[:, :], 0.0).then_inc(buf_zeroed, 1)
            dve.wait_ge(buf_zeroed, 10)
            for e in range(2):
                dve.memset(pick[EMB * e:EMB * e + EMB, e:e + 1], 1.0).then_inc(buf_zeroed, 1)

            def spread(u, a):
                part = slice(FP * a, FP * a + FP)
                return dve.tensor_copy(pt_bd[u % 2][part, :, a, 0:FIELDS], pt_sb[part, :, 0:FIELDS])

            def slot(it, s):
                u1, n1, there1 = unit(it, s + SCORE)
                u2, n2, there2 = unit(it, s + SCORE - 1)
                wide = [PE_ROWS, QUADS * BLOCKS, FIELDS]
                scores = s_ps[:, 0:COLS].rearrange("p (m k) -> p m k", k=FIELDS)
                if there1:
                    wait(dve, s_done, n1 + 1)
                    dve.tensor_reduce(row_max[:, :], scores, AX, ALU.max).then_inc(max_done, 1)
                if there2:
                    wait(dve, p_ready, n2 + 1)
                    dve.transpose(pt_sb[:, :, :], p_sb[:, :, :]).then_inc(pt_done, 1)
                if there1:
                    wait(dve, max_done, n1 + 1)
                    dve.tensor_tensor(e_sb[u1 % 2][:, :, :], scores, row_max[:, :].unsqueeze(2).to_broadcast(wide),
                                      ALU.subtract).then_inc(sub_done, 1)
                if there2:
                    wait(dve, pt_done, n2 + 1)
                    wait(dve, o_done, n2 - 1)
                    for a in range(4):
                        last = spread(u2, a)
                    last.then_inc(pt_ready, 1)
                if there1:
                    e = e_sb[u1 % 2]
                    wait(dve, exp_done, n1 + 1)
                    dve.tensor_reduce(row_sum[:, :], e[:, :, :], AX, ALU.add).then_inc(sum_done, 1)
                    wait(dve, sum_done, n1 + 1)
                    dve.reciprocal(row_inv[:, :], row_sum[:, :]).then_inc(inv_done, 1)
                    wait(dve, inv_done, n1 + 1)
                    wait(dve, pt_ready, n1)
                    dve.tensor_tensor(p_sb[:, :, 0:FIELDS], e[:, :, :], row_inv[:, :].unsqueeze(2).to_broadcast(wide),
                                      ALU.mult).then_inc(p_ready, 1)

                u, n, there = unit(it, s - 1)
                if there and u >= (LAYERS - 1) * CHUNKS:
                    c = u % CHUNKS
                    count = turn(it, s - 1)[0] * CHUNKS + (c + 1)
                    wait(dve, x_ready, n + 1)
                    dve.wait_ge(dnn_w_loaded, DNN_LOADS)
                    wait(dve, att_done, count - 1)
                    dve.tensor_tensor(weighed[:, :, :], x[:, c, :, 0:FIELDS],
                                      ow_att_sb[:, :].unsqueeze(1).to_broadcast([PE_ROWS, CHUNK, FIELDS]),
                                      ALU.mult).then_inc(weighed_done, 1)
                    wait(dve, weighed_done, count)
                    if c == 0:
                        wait(dve, final_done, turn(it, s - 1)[0])
                    dve.tensor_reduce(att_part[:, c * CHUNK:(c + 1) * CHUNK], weighed[:, :, :], AX, ALU.add).then_inc(att_done, 1)

                i, there = turn(it, s, back=1)
                if there and s % UNITS == SUM_SLOT:
                    wait(dve, lin_ready, i + 1)
                    dve.tensor_tensor(logit[:, :], t_ps[0:2, PAIRS:2 * PAIRS], lin[:, :], ALU.add).then_inc(logit_ready, 1)
                if there and s % UNITS == SIGMOID_SLOT:
                    wait(dve, expneg_ready, i + 1)
                    dve.tensor_scalar(denom[:, :], expneg[:, :], 1.0, None, ALU.add).then_inc(denom_ready, 1)
                    wait(dve, denom_ready, i + 1)
                    wait(dve, stored, i * 16)
                    dve.reciprocal(result[:, :], denom[:, :]).then_inc(result_ready, 1)

            over_slots(dve, slot)


_NAMES = ["table", "idx", "offs", "xt", "wq", "wk", "wv", "wr", "w1", "b1", "w2", "b2", "ow_att", "ow_dnn", "lw", "lb"]


def kernel(**inputs):
    import concourse.bacc as _bacc
    from concourse.bass_utils import run_bass_kernel_spmd as _run

    g = {k.replace("L0_rec_", ""): np.asarray(v) for k, v in inputs.items()}
    idx = g["r_sparse_idx"].reshape(ITERATIONS, 2, PAIRS // 4, 4, FIELDS)
    att = FIELDS * EMB
    laid = {
        "table": g["emb_tables"].reshape(FIELDS * VOCAB, EMB),
        "idx": idx.transpose(3, 4, 0, 2, 1).reshape(QCOLS, ITERATIONS, PAIRS // 4 * 2),
        "offs": np.tile(np.arange(FIELDS, dtype=np.int32) * VOCAB, 4).reshape(QCOLS, 1),
        "xt": g["r_X"].reshape(ITERATIONS, 2, PAIRS, FEATURES).transpose(0, 3, 1, 2),
        "wq": g["Wq"], "wk": g["Wk"], "wv": g["Wv"], "wr": g["Wres"],
        "w1": g["dnn_W1"], "b1": g["dnn_b1"].reshape(2, PE_ROWS).T,
        "w2": g["dnn_W2"], "b2": g["dnn_b2"].reshape(HIDDEN2, 1),
        "ow_att": g["out_W"][:att].reshape(FIELDS, EMB).T, "ow_dnn": g["out_W"][att:],
        "lw": g["lin_W"], "lb": g["lin_b"].reshape(1, 1),
    }
    nc = _bacc.Bacc("TRN2", target_bir_lowering=False, num_devices=1)
    arrays, args = {}, []
    for name in _NAMES:
        a = np.ascontiguousarray(laid[name])
        arrays[f"in_{name}"] = a
        args.append(nc.dram_tensor(f"in_{name}", a.shape, mybir.dt.from_np(a.dtype), kind="ExternalInput").ap())
    out = nc.dram_tensor("out", (ITERATIONS, 2, PAIRS), mybir.dt.float32, kind="ExternalOutput").ap()
    interacting_attention_recommender(nc, *args, out)
    r = _run(nc, [arrays], core_ids=[0])
    return np.asarray(r.results[0]["out"]).reshape(BATCH, 1)
```

```python
import numpy as np
import concourse.bass as bass
from concourse import mybir
from contextlib import ExitStack

BATCH, FIELDS, DENSE, VOCAB, EMB = 16384, 26, 13, 10000, 64
HEADS, LAYERS, HIDDEN1, HIDDEN2 = 2, 3, 256, 128
FEATURES = FIELDS + DENSE
HD = EMB // HEADS
PE_ROWS = 128
FP = 32
PAIRS = 128
EXAMPLES = 2 * PAIRS
ITERATIONS = BATCH // EXAMPLES
CHUNK = 16
CHUNKS = PAIRS // CHUNK
QUADS = CHUNK // 4
BLOCKS = 4
COLS = CHUNK * FIELDS
QCOLS = 4 * FIELDS
UNITS = LAYERS * CHUNKS
PROJ, SCORE, PROB, SPREAD, VALUE = 4, 3, 2, 1, 1
FIRST = -PROJ - 4
TURN = CHUNKS - PROJ + 2
VSLOTS = 3
PSLOTS = 3
TWINS = FIELDS // 2
PRODUCTS = 2 * (TWINS + 1)
DNN_SLOT, PER_SLOT = TURN, 2
H1_SLOT = DNN_SLOT + -(-PRODUCTS // PER_SLOT) - 1
X0_SLOT = (LAYERS - 1) * CHUNKS - PROJ + 2
L2_SLOT = X0_SLOT + CHUNKS
WEIGH = 3
FINAL_SLOT, SIGMOID_SLOT = 4, 5


def interacting_attention_recommender(nc, table, idx, offs, xt, wq, wk, wv, wr, w1, b1, w2, b2,
                                      ow_att, ow_dnn, lw, lb, out):
    fp32, fp32r, i32 = mybir.dt.float32, mybir.dt.float32r, mybir.dt.int32
    ALU = mybir.AluOpType
    ACT = mybir.ActivationFunctionType
    AX = mybir.AxisListType.X

    ctx = ExitStack()
    with ctx:
        def sb(name, shape, dt=fp32):
            return ctx.enter_context(nc.sbuf_tensor(name, shape, dt))

        def bank(name):
            return ctx.enter_context(nc.psum_tensor(name, [PE_ROWS, 512], fp32))

        def sem(name):
            return ctx.enter_context(nc.semaphore(name))

        w_att = sb("w_att", [PE_ROWS, LAYERS, 2, PE_ROWS])
        w_qk = sb("w_qk", [PE_ROWS, LAYERS, PE_ROWS])
        w_qk_parts = sb("w_qk_parts", [PE_ROWS, 2, LAYERS, PE_ROWS], fp32r)
        w1_emb = sb("w1_emb", [PE_ROWS, TWINS, HIDDEN1])
        w1_den = sb("w1_den", [DENSE, HIDDEN1])
        w2_sb = sb("w2_sb", [PE_ROWS, 2, HIDDEN2])
        b1_sb = sb("b1_sb", [PE_ROWS, 2])
        b2_sb = sb("b2_sb", [PE_ROWS, 1])
        ow_att_sb = sb("ow_att_sb", [PE_ROWS, FIELDS])
        ow_dnn_sb = sb("ow_dnn_sb", [PE_ROWS, 2, 2])
        lw_sb = sb("lw_sb", [FEATURES, 2, 2])
        lb_sb = sb("lb_sb", [2, 1])
        pick = sb("pick", [PE_ROWS, 2])
        ident = sb("ident", [PE_ROWS, PE_ROWS])
        idx_in = sb("idx_in", [QCOLS, PAIRS // 4 * 2], i32)
        offs_sb = sb("offs_sb", [QCOLS, 1], i32)
        idx_now = sb("idx_now", [QCOLS, PAIRS // 4 * 2], i32)
        rows = sb("rows", [QCOLS, PAIRS // 4, PE_ROWS])
        x0 = sb("x0", [PE_ROWS, CHUNKS, CHUNK, FP])
        x_dnn = sb("x_dnn", [PE_ROWS, TWINS, 2, CHUNKS, CHUNK])
        x = sb("x", [PE_ROWS, CHUNKS, CHUNK, FP])
        x_parts = sb("x_parts", [PE_ROWS, CHUNKS, 2, COLS], fp32r)
        high = [sb(f"high{i}", [PE_ROWS, COLS], fp32r) for i in range(PSLOTS)]
        low = [sb(f"low{i}", [PE_ROWS, COLS], fp32r) for i in range(PSLOTS)]
        high0 = [sb(f"high0_{i}", [PE_ROWS, COLS], fp32r) for i in range(PSLOTS)]
        low0 = [sb(f"low0_{i}", [PE_ROWS, COLS], fp32r) for i in range(PSLOTS)]
        q_sb = [sb(f"q_sb{i}", [PE_ROWS, CHUNK, FP]) for i in range(2)]
        k_bd = [sb(f"k_bd{i}", [PE_ROWS, CHUNK, BLOCKS, FIELDS]) for i in range(2)]
        v_sb = [sb(f"v_sb{i}", [PE_ROWS, QUADS, PE_ROWS]) for i in range(VSLOTS)]
        e_sb = [sb(f"e_sb{i}", [PE_ROWS, QUADS * BLOCKS, FIELDS]) for i in range(2)]
        pt_sb = sb("pt_sb", [PE_ROWS, QUADS * BLOCKS, FP])
        p_sb = sb("p_sb", [PE_ROWS, QUADS * BLOCKS, FP])
        pt_bd = [sb(f"pt_bd{i}", [PE_ROWS, QUADS * BLOCKS, 4, FP]) for i in range(2)]
        row_max = sb("row_max", [PE_ROWS, QUADS * BLOCKS])
        row_sum = sb("row_sum", [PE_ROWS, QUADS * BLOCKS])
        row_inv = sb("row_inv", [PE_ROWS, QUADS * BLOCKS])
        weighed = [sb(f"weighed{i}", [PE_ROWS, CHUNK, FIELDS]) for i in range(2)]
        att_part = sb("att_part", [PE_ROWS, PAIRS])
        x_den = sb("x_den", [DENSE, 2, PAIRS])
        x_all = sb("x_all", [FEATURES, 2, PAIRS])
        h1 = sb("h1", [PE_ROWS, 2, 2, PAIRS])
        h2 = sb("h2", [PE_ROWS, 2, PAIRS])
        lin = sb("lin", [2, PAIRS])
        logit = sb("logit", [2, PAIRS])
        expneg = sb("expneg", [2, PAIRS])
        denom = sb("denom", [2, PAIRS])
        result = sb("result", [2, PAIRS])

        qk_ps = [bank("qk_ps0"), bank("qk_ps1")]
        v_ps, s_ps, o_ps, t_ps = (bank(n) for n in ("v_ps", "s_ps", "o_ps", "t_ps"))
        d_ps = [bank("d_ps0"), bank("d_ps1")]

        w_zeroed = sem("w_zeroed")
        buf_zeroed = sem("buf_zeroed")
        ident_ready = sem("ident_ready")
        att_w_loaded = sem("att_w_loaded")
        dnn_w_loaded = sem("dnn_w_loaded")
        offs_loaded = sem("offs_loaded")
        idx_loaded = sem("idx_loaded")
        w_parts_ready = sem("w_parts_ready")
        idx_ready = sem("idx_ready")
        gathered = [sem(f"gathered{c}") for c in range(CHUNKS)]
        x_den_loaded = sem("x_den_loaded")
        x_all_loaded = sem("x_all_loaded")
        xt_done = sem("xt_done")
        x0_ready = sem("x0_ready")
        x_dnn_ready = sem("x_dnn_ready")
        low0_ready = sem("low0_ready")
        low_ready = sem("low_ready")
        parts_ready = [sem(f"parts_ready{c}") for c in range(CHUNKS)]
        qk_done, v_done = sem("qk_done"), sem("v_done")
        qk_ready, v_ready = sem("qk_ready"), sem("v_ready")
        s_done = sem("s_done")
        max_done, sub_done = sem("max_done"), sem("sub_done")
        exp_done = sem("exp_done")
        sum_done, inv_done, p_ready = sem("sum_done"), sem("inv_done"), sem("p_ready")
        pt_done = sem("pt_done")
        pt_ready = sem("pt_ready")
        o_done = sem("o_done")
        x_ready = sem("x_ready")
        weighed_done, att_done = sem("weighed_done"), sem("att_done")
        dnn_done = sem("dnn_done")
        h1_ready = sem("h1_ready")
        l2_done = sem("l2_done")
        h2_ready = sem("h2_ready")
        final_done = sem("final_done")
        lin_ready, logit_ready, expneg_ready = sem("lin_ready"), sem("logit_ready"), sem("expneg_ready")
        denom_ready, result_ready = sem("denom_ready"), sem("result_ready")
        stored = sem("stored")
        cleared, sp_cleared = sem("cleared"), sem("sp_cleared")

        def unit(it, s):
            n = it * UNITS + s
            return s % UNITS, n, not isinstance(n, int) or 0 <= n < ITERATIONS * UNITS

        def turn(it, s, back=0):
            i = it + (s // UNITS - back)
            return i, s >= 0 and (not isinstance(i, int) or 0 <= i < ITERATIONS)

        def wait(eng, semaphore, value):
            if not isinstance(value, int) or value > 0:
                eng.wait_ge(semaphore, value)

        def embedded(it, s, late):
            if 0 <= s - late - FIRST < CHUNKS and isinstance(it, int) and it == 0:
                yield 0, s - late - FIRST
            u = (s - late) % UNITS
            i, there = turn(it, s - late, back=-1)
            if there and X0_SLOT <= u < X0_SLOT + CHUNKS:
                yield i, u - X0_SLOT

        def inputs(it, s):
            return (it + s // UNITS) * ((LAYERS - 1) * CHUNKS) + (s % UNITS + 1)

        def over_slots(eng, slot):
            for s in range(FIRST, TURN):
                slot(0, s)
            with eng.Fori(0, ITERATIONS - 1) as it:
                for s in range(TURN, TURN + UNITS):
                    slot(it, s)
            for s in range(TURN, TURN + UNITS):
                slot(ITERATIONS - 1, s)

        DNN_LOADS = 16 * 14

        block = ctx.enter_context(nc.Block())

        @block.sync
        def _(sp):
            sp.dma_start(idx_in[:, :], idx[:, 0, :]).then_inc(idx_loaded, 16)
            sp.dma_start(offs_sb[:, :], offs).then_inc(offs_loaded, 16)
            halves = [slice(EMB * e, EMB * e + EMB) for e in range(2)]
            for half in halves:
                for kind, w in enumerate((wq, wk)):
                    sp.dma_start(w_qk[half, :, halves[kind]], w.rearrange("l f o -> f l o")).then_inc(att_w_loaded, 16)
            sp.wait_ge(w_zeroed, 3)
            for half in halves:
                for kind, w in enumerate((wv, wr)):
                    sp.dma_start(w_att[half, :, kind, half], w.rearrange("l f o -> f l o")).then_inc(att_w_loaded, 16)
            for e, half in enumerate(halves):
                sp.dma_start(w1_emb[half, :, :], w1[DENSE:, :].rearrange("(i t f) o -> t f i o", t=2, f=EMB)[e]).then_inc(dnn_w_loaded, 16)
                sp.dma_start(ow_att_sb[half, :], ow_att).then_inc(dnn_w_loaded, 16)
                sp.dma_start(ow_dnn_sb[:, e, e:e + 1], ow_dnn).then_inc(dnn_w_loaded, 16)
                sp.dma_start(lw_sb[:, e, e:e + 1], lw).then_inc(dnn_w_loaded, 16)
                sp.dma_start(lb_sb[e:e + 1, :], lb).then_inc(dnn_w_loaded, 16)
            sp.dma_start(w1_den[:, :], w1[0:DENSE, :]).then_inc(dnn_w_loaded, 16)
            sp.dma_start(x_den[:, :, :], xt[0, FIELDS:, :, :]).then_inc(x_den_loaded, 16)
            sp.dma_start(w2_sb[:, :, :], w2.rearrange("(k p) o -> p k o", p=PE_ROWS)).then_inc(dnn_w_loaded, 16)
            sp.dma_start(b1_sb[:, :], b1).then_inc(dnn_w_loaded, 16)
            sp.dma_start(b2_sb[:, :], b2).then_inc(dnn_w_loaded, 16)
            sp.dma_start(x_all[:, :, :], xt[0]).then_inc(x_all_loaded, 16)

            def move(c, of_high, of_low):
                for e, half in enumerate(halves):
                    sp.dma_start(x_parts[half, c, e, :].bitcast(fp32), of_high[half, :].bitcast(fp32)).then_inc(parts_ready[c], 16)
                    sp.dma_start(x_parts[halves[1 - e], c, e, :].bitcast(fp32), of_low[half, :].bitcast(fp32)).then_inc(parts_ready[c], 16)

            def slot(it, s):
                i, there = turn(it, s, back=-1)
                if there and s % UNITS == TURN:
                    wait(sp, idx_ready, i)
                    sp.sem_inc(sp_cleared, 1)
                    sp.dma_start(idx_in[:, :], idx[:, i, :]).then_inc(idx_loaded, 16)

                for i, c in embedded(it, s, 1):
                    wait(sp, low0_ready, i * CHUNKS + (c + 1))
                    sp.sem_inc(sp_cleared, 1)
                    move(c, high0[c % PSLOTS], low0[c % PSLOTS])
                u, n, there = unit(it, s - 1)
                if there and u < (LAYERS - 1) * CHUNKS:
                    wait(sp, low_ready, inputs(it, s - 1))
                    sp.sem_inc(sp_cleared, 1)
                    move(u % CHUNKS, high[u % PSLOTS], low[u % PSLOTS])

                i, there = turn(it, s, back=-1)
                if there and s % UNITS == H1_SLOT + 1:
                    wait(sp, dnn_done, i)
                    sp.sem_inc(sp_cleared, 1)
                    sp.dma_start(x_den[:, :, :], xt[i, FIELDS:, :, :]).then_inc(x_den_loaded, 16)

                i, there = turn(it, s, back=1)
                if there and s % UNITS == SIGMOID_SLOT:
                    wait(sp, result_ready, i + 1)
                    sp.sem_inc(sp_cleared, 1)
                    sp.dma_start(out[i], result[:, :]).then_inc(stored, 16)
                    if not isinstance(i, int) or i + 1 < ITERATIONS:
                        wait(sp, stored, (i + 1) * 16)
                        sp.sem_inc(sp_cleared, 1)
                        sp.dma_start(x_all[:, :, :], xt[i + 1]).then_inc(x_all_loaded, 16)

            over_slots(sp, slot)
            sp.wait_ge(stored, 16 * ITERATIONS)

        @block.gpsimd
        def _(pool):
            pool.memset(w_att[:, :, :, :], 0.0).then_inc(w_zeroed, 1)
            pool.memset(ow_dnn_sb[:, :, :], 0.0).then_inc(w_zeroed, 1)
            pool.memset(lw_sb[:, :, :], 0.0).then_inc(w_zeroed, 1)
            pool.memset(ident[:, :], 0.0).then_inc(ident_ready, 1)
            pool.wait_ge(ident_ready, 1)
            pool.affine_select(out=ident[:, :], in_=ident[:, :], compare_op=ALU.not_equal, fill=1.0,
                               base=0, pattern=[[-1, PE_ROWS]], channel_multiplier=1).then_inc(ident_ready, 1)
            pool.wait_ge(offs_loaded, 16)

            def twin(it, c):
                wait(pool, x0_ready, it * CHUNKS + (c + 1))
                wait(pool, dnn_done, it)
                pool.sem_inc(cleared, 1)
                for e in range(2):
                    twins = x0[EMB * e:EMB * e + EMB, c, :, 0:FIELDS].rearrange("p n (i t) -> p t i n", t=2)
                    for t in range(2):
                        pool.tensor_copy(x_dnn[EMB * t:EMB * t + EMB, :, e, c, :], twins[:, t, :, :]).then_inc(x_dnn_ready, 1)
                        pool.wait_ge(x_dnn_ready, it * CHUNKS * 4 + (4 * c + 2 * e + t + 1))
                        pool.sem_inc(cleared, 1)

            def weigh(it, c):
                wait(pool, x_ready, it * UNITS + ((LAYERS - 1) * CHUNKS + c + 1))
                pool.wait_ge(dnn_w_loaded, DNN_LOADS)
                if c >= 2:
                    wait(pool, att_done, it * CHUNKS + (c - 1))
                pool.sem_inc(cleared, 1)
                pool.tensor_tensor(weighed[c % 2][:, :, :], x[:, c, :, 0:FIELDS],
                                   ow_att_sb[:, :].unsqueeze(1).to_broadcast([PE_ROWS, CHUNK, FIELDS]),
                                   ALU.mult).then_inc(weighed_done, 1)
                pool.wait_ge(weighed_done, it * CHUNKS + (c + 1))
                pool.sem_inc(cleared, 1)

            def gather(it, first):
                wait(pool, idx_loaded, (it + 1) * 16)
                pool.tensor_tensor(idx_now[:, :], idx_in[:, :], offs_sb[:, :].to_broadcast([QCOLS, PAIRS // 4 * 2]),
                                   ALU.add).then_inc(idx_ready, 1)
                pool.wait_ge(idx_ready, it + 1)
                pool.sem_inc(cleared, 1)
                for c in range(CHUNKS):
                    if not first:
                        pool.wait_ge(xt_done, it * CHUNKS + (c + 1 - CHUNKS))
                    pool.sem_inc(cleared, 1)
                    for g in range(c * QUADS, (c + 1) * QUADS):
                        for e in range(2):
                            pool.indirect_dma_start(
                                out=rows[:, g, EMB * e:EMB * e + EMB], out_offset=None, in_=table,
                                in_offset=bass.IndirectOffsetOnAxis(ap=idx_now[:, 2 * g + e:2 * g + e + 1], axis=0),
                            ).then_inc(gathered[c], 16)
                for c in range(CHUNKS):
                    pool.wait_ge(gathered[c], (it + 1) * (16 * 2 * QUADS))
                    pool.sem_inc(cleared, 1)

            gather(0, True)
            for c in range(CHUNKS):
                twin(0, c)
            with pool.Fori(1, ITERATIONS) as it:
                gather(it, False)
                weigh(it - 1, 0)
                for c in range(CHUNKS):
                    if c + 1 < CHUNKS:
                        weigh(it - 1, c + 1)
                    twin(it, c)
            for c in range(CHUNKS):
                weigh(ITERATIONS - 1, c)

        @block.tensor
        def _(pe):
            def embed(it, c):
                wait(pe, gathered[c], (it + 1) * (16 * 2 * QUADS))
                wait(pe, x0_ready, it * CHUNKS + c)
                for g in range(QUADS):
                    last = pe.transpose(t_ps[:, g * QCOLS:(g + 1) * QCOLS], rows[:, c * QUADS + g, :], ident[0:QCOLS, 0:QCOLS])
                last.then_inc(xt_done, 1)

            pe.wait_ge(ident_ready, 2)
            pe.wait_ge(att_w_loaded, 16 * 8)
            pe.wait_ge(w_parts_ready, 2)

            def slot(it, s):
                u, n, there = unit(it, s + PROJ)
                if there:
                    l, c = divmod(u, CHUNKS)
                    if l:
                        wait(pe, x_ready, n + (1 - CHUNKS))
                    else:
                        wait(pe, x0_ready, turn(it, s + PROJ)[0] * CHUNKS + (c + 1))
                    wait(pe, parts_ready[c], (turn(it, s + PROJ)[0] * LAYERS + (l + 1)) * 64)
                    wait(pe, qk_ready, n)
                    for part in range(2):
                        for e in range(2):
                            last = pe.matmul(qk_ps[e][:, 0:COLS], w_qk_parts[:, part, l, :], x_parts[:, c, e, :],
                                             start=part == 0, stop=part == 1)
                    last.then_inc(qk_done, 1)

                u, n, there = unit(it, s + VALUE)
                if there:
                    l, c = divmod(u, CHUNKS)
                    src = x if l else x0
                    wait(pe, v_ready, n)
                    for g in range(QUADS):
                        last = pe.matmul(v_ps[:, g * PE_ROWS:(g + 1) * PE_ROWS], src[:, c, 4 * g:4 * g + 4, :],
                                         w_att[:, l, 0, :], start=True, stop=True)
                    last.then_inc(v_done, 1)

                u, n, there = unit(it, s)
                if there:
                    l, c = divmod(u, CHUNKS)
                    src = x if l else x0
                    wait(pe, x_ready, n)
                    pe.matmul(o_ps[:, 0:COLS], w_att[:, l, 1, :], src[:, c, :, 0:FIELDS], start=True, stop=False,
                              skip_group_check=True)

                u = s % UNITS
                i, there = turn(it, s)
                if there and DNN_SLOT <= u <= H1_SLOT:
                    if u == DNN_SLOT:
                        pe.wait_ge(dnn_w_loaded, DNN_LOADS)
                        wait(pe, x_dnn_ready, (i + 1) * (4 * CHUNKS))
                        wait(pe, x_den_loaded, (i + 1) * 16)
                    done = (u - DNN_SLOT) * PER_SLOT
                    for product in range(done, min(done + PER_SLOT, PRODUCTS)):
                        half, t = divmod(product, TWINS + 1)
                        hidden = slice(half * PE_ROWS, (half + 1) * PE_ROWS)
                        if t < TWINS:
                            last = pe.matmul(d_ps[half][:, 0:EXAMPLES], w1_emb[:, t, hidden],
                                             x_dnn[:, t, :, :, :].rearrange("p e c n -> p (e c n)"), start=t == 0, stop=False)
                        else:
                            last = pe.matmul(d_ps[half][:, 0:EXAMPLES], w1_den[:, hidden],
                                             x_den[:, :, :].rearrange("p e n -> p (e n)"), start=False, stop=True)
                    if u == H1_SLOT:
                        last.then_inc(dnn_done, 1)

                if there and u == L2_SLOT:
                    wait(pe, h1_ready, i + 1)
                    if not isinstance(i, int) or i + 1 < ITERATIONS:
                        wait(pe, x0_ready, i * CHUNKS + 2 * CHUNKS)
                    for k in range(2):
                        last = pe.matmul(t_ps[:, 0:EXAMPLES], w2_sb[:, k, :], h1[:, k, :, :], start=k == 0, stop=k == 1)
                    last.then_inc(l2_done, 1)

                for i, c in embedded(it, s, 0):
                    embed(i, c)

                i, there = turn(it, s, back=1)
                if there and s % UNITS == FINAL_SLOT:
                    wait(pe, x_all_loaded, (i + 1) * 16)
                    wait(pe, att_done, (i + 1) * CHUNKS)
                    wait(pe, h2_ready, i + 1)
                    pe.matmul(t_ps[0:2, PAIRS:2 * PAIRS], pick[:, :], att_part[:, :], start=True, stop=False)
                    for e in range(2):
                        pe.matmul(t_ps[0:2, PAIRS:2 * PAIRS], ow_dnn_sb[:, e, :], h2[:, e, :], start=False, stop=e == 1)
                    for e in range(2):
                        last = pe.matmul(t_ps[0:2, 0:PAIRS], lw_sb[:, e, :], x_all[:, e, :], start=e == 0, stop=e == 1)
                    last.then_inc(final_done, 1)

                u, n, there = unit(it, s + SCORE)
                if there:
                    wait(pe, qk_ready, n + 1)
                    wait(pe, sub_done, n)
                    for p in range(CHUNK):
                        g, a = divmod(p, 4)
                        last = pe.matmul(s_ps[FP * a:FP * a + FP, g * QCOLS:(g + 1) * QCOLS], q_sb[u % 2][:, p, :],
                                         k_bd[u % 2][:, p, :, :], start=True, stop=True)
                    last.then_inc(s_done, 1)

                u, n, there = unit(it, s)
                if there:
                    wait(pe, v_ready, n + 1)
                    wait(pe, pt_ready, n + 1)
                    for g in range(QUADS):
                        for b in range(BLOCKS):
                            last = pe.matmul(o_ps[FP * b:FP * b + FP, g * QCOLS:(g + 1) * QCOLS],
                                             v_sb[u % VSLOTS][:, g, HD * b:HD * b + HD],
                                             pt_bd[u % 2][:, g * BLOCKS + b, :, 0:FIELDS], start=False, stop=True,
                                             skip_group_check=True)
                    last.then_inc(o_done, 1)

            over_slots(pe, slot)

        @block.scalar
        def _(act):
            def embed(it, c):
                wait(act, xt_done, it * CHUNKS + (c + 1))
                if c >= PSLOTS:
                    wait(act, parts_ready[c - PSLOTS], (it * LAYERS + 1) * 64)
                act.activation(high0[c % PSLOTS][:, :], t_ps[:, 0:COLS], ACT.Copy)
                act.activation(x0[:, c, :, 0:FIELDS], t_ps[:, 0:COLS].rearrange("p (n f) -> p n f", f=FIELDS),
                               ACT.Copy).then_inc(x0_ready, 1)

            act.wait_ge(buf_zeroed, 5)

            def slot(it, s):
                u, n, there = unit(it, s + PROJ)
                if there:
                    wait(act, qk_done, n + 1)
                    wait(act, s_done, n - 1)
                    for e in range(2):
                        act.activation(q_sb[u % 2][EMB * e:EMB * e + EMB, :, 0:FIELDS],
                                       qk_ps[e][0:EMB, 0:COLS].rearrange("p (n f) -> p n f", f=FIELDS), ACT.Copy)
                    for b in range(BLOCKS):
                        e, h = divmod(b, HEADS)
                        keys = qk_ps[e][EMB + HD * h:EMB + HD * h + HD, 0:COLS].rearrange("p (n f) -> p n f", f=FIELDS)
                        last = act.activation(k_bd[u % 2][FP * b:FP * b + FP, :, b, :], keys, ACT.Copy)
                    last.then_inc(qk_ready, 1)

                u, n, there = unit(it, s + PROB)
                if there:
                    wait(act, sub_done, n + 1)
                    act.activation(e_sb[u % 2][:, :, :], e_sb[u % 2][:, :, :], ACT.Exp).then_inc(exp_done, 1)

                u, n, there = unit(it, s + VALUE)
                if there:
                    wait(act, v_done, n + 1)
                    wait(act, o_done, n + (1 - VSLOTS))
                    act.activation(v_sb[u % VSLOTS][:, :, :].rearrange("p g n -> p (g n)"), v_ps[:, :], ACT.Copy).then_inc(v_ready, 1)

                i, there = turn(it, s, back=1)
                if there and s % UNITS == FINAL_SLOT:
                    wait(act, final_done, i + 1)
                    act.activation(lin[:, :], t_ps[0:2, 0:PAIRS], ACT.Relu, bias=lb_sb[:, 0:1]).then_inc(lin_ready, 1)

                u, n, there = unit(it, s)
                if there:
                    c = u % CHUNKS
                    act.wait_ge(buf_zeroed, 10)
                    wait(act, o_done, n + 1)
                    if u < (LAYERS - 1) * CHUNKS:
                        if u >= PSLOTS:
                            l2, c2 = divmod(u - PSLOTS, CHUNKS)
                            wait(act, parts_ready[c2], (turn(it, s)[0] * LAYERS + (l2 + 2)) * 64)
                        act.activation(high[u % PSLOTS][:, :], o_ps[:, 0:COLS], ACT.Relu)
                    act.activation(x[:, c, :, 0:FIELDS], o_ps[:, 0:COLS].rearrange("p (n f) -> p n f", f=FIELDS),
                                   ACT.Relu).then_inc(x_ready, 1)

                i, there = turn(it, s)
                if there and u == H1_SLOT:
                    wait(act, dnn_done, i + 1)
                    act.wait_ge(dnn_w_loaded, DNN_LOADS)
                    for half in range(2):
                        last = act.activation(h1[:, half, :, :].rearrange("p e n -> p (e n)"), d_ps[half][:, 0:EXAMPLES],
                                              ACT.Relu, bias=b1_sb[:, half:half + 1])
                    last.then_inc(h1_ready, 1)
                if there and u == L2_SLOT:
                    wait(act, l2_done, i + 1)
                    act.activation(h2[:, :, :].rearrange("p e n -> p (e n)"), t_ps[:, 0:EXAMPLES], ACT.Relu,
                                   bias=b2_sb[:, 0:1]).then_inc(h2_ready, 1)

                for i, c in embedded(it, s, 0):
                    embed(i, c)

                i, there = turn(it, s, back=1)
                if there and s % UNITS == SIGMOID_SLOT:
                    wait(act, logit_ready, i + 1)
                    act.activation(expneg[:, :], logit[:, :], ACT.Exp, scale=-1.0).then_inc(expneg_ready, 1)

            over_slots(act, slot)

        @block.vector
        def _(dve):
            dve.memset(x0[:, :, :, :], 0.0).then_inc(buf_zeroed, 1)
            for t in q_sb:
                dve.memset(t[:, :, :], 0.0).then_inc(buf_zeroed, 1)
            for t in k_bd:
                dve.memset(t[:, :, :, :], 0.0).then_inc(buf_zeroed, 1)
            dve.memset(x[:, :, :, :], 0.0).then_inc(buf_zeroed, 1)
            dve.memset(p_sb[:, :, :], 0.0).then_inc(buf_zeroed, 1)
            for t in pt_bd:
                dve.memset(t[:, :, :, :], 0.0).then_inc(buf_zeroed, 1)
            dve.memset(pick[:, :], 0.0).then_inc(buf_zeroed, 1)
            dve.wait_ge(buf_zeroed, 10)
            for e in range(2):
                dve.memset(pick[EMB * e:EMB * e + EMB, e:e + 1], 1.0).then_inc(buf_zeroed, 1)

            dve.wait_ge(att_w_loaded, 16 * 8)
            dve.tensor_copy(w_qk_parts[:, 0, :, :], w_qk[:, :, :]).then_inc(w_parts_ready, 1)
            dve.wait_ge(w_parts_ready, 1)
            dve.tensor_tensor(w_qk_parts[:, 1, :, :], w_qk[:, :, :], w_qk_parts[:, 0, :, :].bitcast(fp32),
                              ALU.subtract).then_inc(w_parts_ready, 1)

            def split(whole, of_high, of_low):
                of = [t[:, :].rearrange("p (n f) -> p n f", f=FIELDS) for t in (of_low, of_high)]
                return dve.tensor_tensor(of[0], whole, of[1].bitcast(fp32), ALU.subtract)

            def slot(it, s):
                u1, n1, there1 = unit(it, s + SCORE)
                u2, n2, there2 = unit(it, s + SPREAD)
                u3, n3, there3 = unit(it, s + PROB)
                wide = [PE_ROWS, QUADS * BLOCKS, FIELDS]
                scores = s_ps[:, 0:COLS].rearrange("p (m k) -> p m k", k=FIELDS)
                if there1:
                    wait(dve, s_done, n1 + 1)
                    dve.tensor_reduce(row_max[:, :], scores, AX, ALU.max).then_inc(max_done, 1)
                if there2:
                    wait(dve, p_ready, n2 + 1)
                    wait(dve, pt_ready, n2)
                    dve.transpose(pt_sb[:, :, :], p_sb[:, :, :]).then_inc(pt_done, 1)
                if there1:
                    wait(dve, max_done, n1 + 1)
                    dve.tensor_tensor(e_sb[u1 % 2][:, :, :], scores, row_max[:, :].unsqueeze(2).to_broadcast(wide),
                                      ALU.subtract).then_inc(sub_done, 1)
                if there2:
                    wait(dve, pt_done, n2 + 1)
                    wait(dve, o_done, n2 - 1)
                    for a in range(4):
                        part = slice(FP * a, FP * a + FP)
                        last = dve.tensor_copy(pt_bd[u2 % 2][part, :, a, 0:FIELDS], pt_sb[part, :, 0:FIELDS])
                    last.then_inc(pt_ready, 1)
                if there3:
                    e = e_sb[u3 % 2]
                    wait(dve, exp_done, n3 + 1)
                    dve.tensor_reduce(row_sum[:, :], e[:, :, :], AX, ALU.add).then_inc(sum_done, 1)
                u, n, there = unit(it, s - 1)
                if there and u < (LAYERS - 1) * CHUNKS:
                    wait(dve, x_ready, n + 1)
                    split(x[:, u % CHUNKS, :, 0:FIELDS], high[u % PSLOTS], low[u % PSLOTS]).then_inc(low_ready, 1)
                if there3:
                    wait(dve, sum_done, n3 + 1)
                    dve.reciprocal(row_inv[:, :], row_sum[:, :]).then_inc(inv_done, 1)
                for i, c in embedded(it, s, 1):
                    wait(dve, x0_ready, i * CHUNKS + (c + 1))
                    split(x0[:, c, :, 0:FIELDS], high0[c % PSLOTS], low0[c % PSLOTS]).then_inc(low0_ready, 1)
                if there3:
                    wait(dve, inv_done, n3 + 1)
                    wait(dve, pt_done, n3)
                    dve.tensor_tensor(p_sb[:, :, 0:FIELDS], e[:, :, :], row_inv[:, :].unsqueeze(2).to_broadcast(wide),
                                      ALU.mult).then_inc(p_ready, 1)

                u, n, there = unit(it, s - WEIGH)
                if there and u >= (LAYERS - 1) * CHUNKS:
                    c = u % CHUNKS
                    wait(dve, weighed_done, turn(it, s - WEIGH)[0] * CHUNKS + (c + 1))
                    dve.tensor_reduce(att_part[:, c * CHUNK:(c + 1) * CHUNK], weighed[c % 2][:, :, :], AX, ALU.add).then_inc(att_done, 1)

                i, there = turn(it, s, back=1)
                if there and s % UNITS == FINAL_SLOT:
                    wait(dve, lin_ready, i + 1)
                    dve.tensor_tensor(logit[:, :], t_ps[0:2, PAIRS:2 * PAIRS], lin[:, :], ALU.add).then_inc(logit_ready, 1)
                if there and s % UNITS == SIGMOID_SLOT:
                    wait(dve, expneg_ready, i + 1)
                    dve.tensor_scalar(denom[:, :], expneg[:, :], 1.0, None, ALU.add).then_inc(denom_ready, 1)
                    wait(dve, denom_ready, i + 1)
                    dve.reciprocal(result[:, :], denom[:, :]).then_inc(result_ready, 1)

            over_slots(dve, slot)


_NAMES = ["table", "idx", "offs", "xt", "wq", "wk", "wv", "wr", "w1", "b1", "w2", "b2", "ow_att", "ow_dnn", "lw", "lb"]


def kernel(**inputs):
    import concourse.bacc as _bacc
    from concourse.bass_utils import run_bass_kernel_spmd as _run

    g = {k.replace("L0_rec_", ""): np.asarray(v) for k, v in inputs.items()}
    idx = g["r_sparse_idx"].reshape(ITERATIONS, 2, PAIRS // 4, 4, FIELDS)
    att = FIELDS * EMB
    laid = {
        "table": g["emb_tables"].reshape(FIELDS * VOCAB, EMB),
        "idx": idx.transpose(3, 4, 0, 2, 1).reshape(QCOLS, ITERATIONS, PAIRS // 4 * 2),
        "offs": np.tile(np.arange(FIELDS, dtype=np.int32) * VOCAB, 4).reshape(QCOLS, 1),
        "xt": g["r_X"].reshape(ITERATIONS, 2, PAIRS, FEATURES).transpose(0, 3, 1, 2),
        "wq": g["Wq"], "wk": g["Wk"], "wv": g["Wv"], "wr": g["Wres"],
        "w1": g["dnn_W1"], "b1": g["dnn_b1"].reshape(2, PE_ROWS).T,
        "w2": g["dnn_W2"], "b2": g["dnn_b2"].reshape(HIDDEN2, 1),
        "ow_att": g["out_W"][:att].reshape(FIELDS, EMB).T, "ow_dnn": g["out_W"][att:],
        "lw": g["lin_W"], "lb": g["lin_b"].reshape(1, 1),
    }
    nc = _bacc.Bacc("TRN2", target_bir_lowering=False, num_devices=1)
    arrays, args = {}, []
    for name in _NAMES:
        a = np.ascontiguousarray(laid[name])
        arrays[f"in_{name}"] = a
        args.append(nc.dram_tensor(f"in_{name}", a.shape, mybir.dt.from_np(a.dtype), kind="ExternalInput").ap())
    out = nc.dram_tensor("out", (ITERATIONS, 2, PAIRS), mybir.dt.float32, kind="ExternalOutput").ap()
    interacting_attention_recommender(nc, *args, out)
    r = _run(nc, [arrays], core_ids=[0])
    return np.asarray(r.results[0]["out"]).reshape(BATCH, 1)
```
